# Optimizing a Trainium2 kernel written in Bass

```python
import numpy as np
import jax
import jax.numpy as jnp

def _softmax(x, axis=-1):
    return jax.nn.softmax(x, axis=axis)

def _gelu(x):
    return jax.nn.gelu(x, approximate=True)

def _silu(x):
    return jax.nn.silu(x)

def _sigmoid(x):
    return jax.nn.sigmoid(x)

def _layernorm(x, axis=-1, eps=1e-05):
    m = jnp.mean(x, axis=axis, keepdims=True)
    v = jnp.var(x, axis=axis, keepdims=True)
    return (x - m) / jnp.sqrt(v + eps)

def _scatter_add(tgt, idx, src, axis=0):
    return tgt.at[idx].add(src)

def _segment_sum(src, seg, n):
    return jax.ops.segment_sum(src, seg, n)
kernel_name = 'mk_perceiver_d1_seqx_r4_e643f4'

def setup_inputs(seed: int=0):
    np.random.seed(seed)
    _w = jnp.asarray

    def _rec_inputs():
        import jax
        import jax.numpy as jnp
        _rk = jax.random.key(seed)
        x = 0.0003765 + 1 * jax.random.normal(jax.random.fold_in(_rk, 1), (32, 64, 256), jnp.float32)
        _lenS = 64 - jax.random.randint(jax.random.fold_in(_rk, 7), (32,), 0, max(1, 64 // 4) + 1, jnp.int32)
        _lenS2 = 1601 - jax.random.randint(jax.random.fold_in(_rk, 8), (32,), 0, max(1, 1601 // 4) + 1, jnp.int32)
        _ctx_1024P = jax.random.normal(jax.random.fold_in(_rk, 11), (32, 16, 256), jnp.float32)
        _ctx_1024c = jax.random.dirichlet(jax.random.fold_in(_rk, 511), 0.3 * jnp.ones((16,), jnp.float32), (32, 1601))
        _ctx_1024t = jnp.einsum('bsk,bkd->bsd', _ctx_1024c, _ctx_1024P)
        _ctx_1024t = _ctx_1024t * jax.lax.rsqrt(jnp.mean(jnp.square(_ctx_1024t)) + 1e-12) * 0.953939
        ctx_1024 = 7.22013e-05 + 1.00017 * (_ctx_1024t + 0.3 * jax.random.normal(jax.random.fold_in(_rk, 611), (32, 1601, 256), jnp.float32))
        return (x, ctx_1024, _lenS2)
    x, ctx_1024, _lenS2 = _rec_inputs()

    def _L0_xattn_setup():
        import jax, jax.numpy as jnp
        import numpy as np
        B, LK, LQ, D, H = (4, 512, 256, 256, 16)
        DH = D // H
        NEG = -1e+18
        key = jax.random.key(seed)
        ks = jax.random.split(key, 12)
        s = 1.0 / np.sqrt(D)
        return {'key': jax.random.normal(ks[0], (B, LK, D), jnp.float32), 'value': jax.random.normal(ks[1], (B, LK, D), jnp.float32), 'query': jax.random.normal(ks[2], (B, LQ, D), jnp.float32), 'key_lens': jax.random.randint(ks[3], (B,), 1, LK + 1), 'query_lens': jax.random.randint(ks[4], (B,), 1, LQ + 1), 'Wk': jax.random.normal(ks[5], (D, D), jnp.float32) * s, 'bk': jnp.zeros((D,), jnp.float32), 'Wq': jax.random.normal(ks[6], (D, D), jnp.float32) * s, 'bq': jnp.zeros((D,), jnp.float32), 'Wv': jax.random.normal(ks[7], (D, D), jnp.float32) * s, 'bv': jnp.zeros((D,), jnp.float32)}
    _L0_xattn_all = _L0_xattn_setup()
    _L0_xattn_in = {k: v for k, v in _L0_xattn_all.items() if k in ('Wk', 'bk', 'Wq', 'bq', 'Wv', 'bv')}
    del _L0_xattn_all

    def _L0_attn_setup():
        import jax, jax.numpy as jnp
        import numpy as np
        D = 256
        H = 16
        S = 512
        B = 2
        LN_EPS = 1e-05
        key = jax.random.key(seed)
        ks = jax.random.split(key, 8)
        x = jax.random.normal(ks[0], (B, S, D), dtype=jnp.float32)
        W_w = jax.random.normal(ks[1], (3 * D, D), dtype=jnp.float32) * 0.02
        W_b = jnp.zeros((3 * D,), dtype=jnp.float32)
        proj_w = jax.random.normal(ks[2], (D, D), dtype=jnp.float32) * 0.02
        proj_b = jnp.zeros((D,), dtype=jnp.float32)
        ln_g = jnp.ones((D,), dtype=jnp.float32)
        ln_b = jnp.zeros((D,), dtype=jnp.float32)
        rpb = jax.random.normal(ks[3], (2 * S - 1, H), dtype=jnp.float32)
        return {'x': x, 'W_w': W_w, 'W_b': W_b, 'proj_w': proj_w, 'proj_b': proj_b, 'ln_g': ln_g, 'ln_b': ln_b, 'rpb': rpb}
    _L0_attn_all = _L0_attn_setup()
    _L0_attn_in = {k: v for k, v in _L0_attn_all.items() if k in ('W_w', 'W_b', 'proj_w', 'proj_b', 'ln_g', 'ln_b', 'rpb')}
    del _L0_attn_all

    def _L0_ffn_setup():
        import jax, jax.numpy as jnp
        import numpy as np
        BLOCK = 32
        W_BITS = 4
        ACT_BITS = 16

        def act_qdq(x):
            qmax = 2.0 ** (ACT_BITS - 1) - 1.0
            scale = jnp.maximum(jnp.max(jnp.abs(x)) / qmax, 1e-12)
            return jnp.clip(jnp.round(x / scale), -qmax - 1.0, qmax) * scale

        def fixed_qdq_u16(x):
            scale = 1.0 / 65536.0
            return jnp.clip(jnp.round(x / scale), 0.0, 65535.0) * scale

        def lpbq_dequant(w):
            O, I = w.shape
            qmax = 2.0 ** (W_BITS - 1) - 1.0
            wb = w.reshape(O, I // BLOCK, BLOCK)
            s = jnp.maximum(jnp.max(jnp.abs(wb), axis=-1, keepdims=True) / qmax, 1e-12)
            wq = jnp.clip(jnp.round(wb / s), -qmax - 1.0, qmax) * s
            return wq.reshape(O, I)
        key = jax.random.key(seed)
        k1, k2, k3, k4 = jax.random.split(key, 4)
        B, S, H, I = (2, 1024, 256, 768)
        x = jax.random.normal(k1, (B, S, H), jnp.float32)
        w_gate = jax.random.normal(k2, (I, H), jnp.float32) * 0.02
        w_up = jax.random.normal(k3, (I, H), jnp.float32) * 0.02
        w_down = jax.random.normal(k4, (H, I), jnp.float32) * 0.02
        return {'x': x, 'w_gate': w_gate, 'w_up': w_up, 'w_down': w_down}
    _L0_ffn_all = _L0_ffn_setup()
    _L0_ffn_in = {k: v for k, v in _L0_ffn_all.items() if k in ('w_gate', 'w_up', 'w_down')}
    del _L0_ffn_all
    return {'x': x, 'ctx_1024': ctx_1024, '_lenS2': _lenS2, 'L0_xattn_Wk': _L0_xattn_in['Wk'], 'L0_xattn_bk': _L0_xattn_in['bk'], 'L0_xattn_Wq': _L0_xattn_in['Wq'], 'L0_xattn_bq': _L0_xattn_in['bq'], 'L0_xattn_Wv': _L0_xattn_in['Wv'], 'L0_xattn_bv': _L0_xattn_in['bv'], 'L0_attn_W_w': _L0_attn_in['W_w'], 'L0_attn_W_b': _L0_attn_in['W_b'], 'L0_attn_proj_w': _L0_attn_in['proj_w'], 'L0_attn_proj_b': _L0_attn_in['proj_b'], 'L0_attn_ln_g': _L0_attn_in['ln_g'], 'L0_attn_ln_b': _L0_attn_in['ln_b'], 'L0_attn_rpb': _L0_attn_in['rpb'], 'L0_ffn_w_gate': _L0_ffn_in['w_gate'], 'L0_ffn_w_up': _L0_ffn_in['w_up'], 'L0_ffn_w_down': _L0_ffn_in['w_down']}

def reference(x, ctx_1024, _lenS2, L0_xattn_Wk, L0_xattn_bk, L0_xattn_Wq, L0_xattn_bq, L0_xattn_Wv, L0_xattn_bv, L0_attn_W_w, L0_attn_W_b, L0_attn_proj_w, L0_attn_proj_b, L0_attn_ln_g, L0_attn_ln_b, L0_attn_rpb, L0_ffn_w_gate, L0_ffn_w_up, L0_ffn_w_down):
    import jax
    import jax.numpy as jnp

    def _L0_xattn_ref(key, value, query, key_lens, query_lens, Wk, bk, Wq, bq, Wv, bv):
        import jax, jax.numpy as jnp
        import numpy as np
        B, LK, LQ, D, H = (4, 512, 256, 256, 16)
        DH = D // H
        NEG = -1e+18
        b, lk, d = key.shape
        lq = query.shape[1]
        k = (key @ Wk.T + bk).reshape(b, lk, H, DH)
        v = (value @ Wv.T + bv).reshape(b, lk, H, DH)
        q = (query @ Wq.T + bq).reshape(b, lq, H, DH)
        score = jnp.einsum('bqhd,bkhd->bhqk', q, k) / jnp.sqrt(jnp.float32(DH))
        kmask = jnp.arange(lk)[None, :] < key_lens[:, None]
        qmask = jnp.arange(lq)[None, :] < query_lens[:, None]
        valid = qmask[:, :, None] & kmask[:, None, :]
        score = score + jnp.where(valid, 0.0, NEG)[:, None, :, :]
        attn = jax.nn.softmax(score, axis=-1)
        ctx = jnp.einsum('bhqk,bkhd->bqhd', attn, v).reshape(b, lq, d)
        return ctx

    def _L0_attn_ref(x, W_w, W_b, proj_w, proj_b, ln_g, ln_b, rpb):
        import jax, jax.numpy as jnp
        import numpy as np
        D = 256
        H = 16
        S = 512
        B = 2
        LN_EPS = 1e-05
        b, s, d = x.shape
        hd = d // H
        qkv = x @ W_w.T + W_b
        q, k, v = jnp.split(qkv, 3, axis=-1)
        q, k, v = (z.reshape(b, s, H, hd).transpose(0, 2, 1, 3) for z in (q, k, v))
        attn = jnp.einsum('bhqd,bhkd->bhqk', q, k) / jnp.sqrt(jnp.float32(d))
        causal = jnp.triu(jnp.ones((s, s), dtype=bool), k=1)
        attn = jnp.where(causal[None, None], -jnp.inf, attn)
        rel_idx = jnp.arange(s)[None, :] - jnp.arange(s)[:, None] + (s - 1)
        bias = rpb[rel_idx].transpose(2, 0, 1)
        attn = attn + bias[None]
        w = jax.nn.softmax(attn, axis=-1)
        o = jnp.einsum('bhqk,bhkd->bhqd', w, v)
        o = o.transpose(0, 2, 1, 3).reshape(b, s, d)
        out = o @ proj_w.T + proj_b
        y = x + out
        mu = jnp.mean(y, axis=-1, keepdims=True)
        var = jnp.var(y, axis=-1, keepdims=True)
        return (y - mu) / jnp.sqrt(var + LN_EPS) * ln_g + ln_b

    def _L0_ffn_ref(x, w_gate, w_up, w_down):
        import jax, jax.numpy as jnp
        import numpy as np
        BLOCK = 32
        W_BITS = 4
        ACT_BITS = 16

        def act_qdq(x):
            qmax = 2.0 ** (ACT_BITS - 1) - 1.0
            scale = jnp.maximum(jnp.max(jnp.abs(x)) / qmax, 1e-12)
            return jnp.clip(jnp.round(x / scale), -qmax - 1.0, qmax) * scale

        def fixed_qdq_u16(x):
            scale = 1.0 / 65536.0
            return jnp.clip(jnp.round(x / scale), 0.0, 65535.0) * scale

        def lpbq_dequant(w):
            O, I = w.shape
            qmax = 2.0 ** (W_BITS - 1) - 1.0
            wb = w.reshape(O, I // BLOCK, BLOCK)
            s = jnp.maximum(jnp.max(jnp.abs(wb), axis=-1, keepdims=True) / qmax, 1e-12)
            wq = jnp.clip(jnp.round(wb / s), -qmax - 1.0, qmax) * s
            return wq.reshape(O, I)
        x = act_qdq(x)
        up = act_qdq(x @ lpbq_dequant(w_up).T)
        gate = act_qdq(x @ lpbq_dequant(w_gate).T)
        sig = fixed_qdq_u16(jax.nn.sigmoid(gate))
        gate = act_qdq(gate * sig)
        o = act_qdq(gate * up)
        return o @ lpbq_dequant(w_down).T
    x = x + _L0_xattn_ref(ctx_1024, ctx_1024, _layernorm(x, axis=-1), _lenS2, _lenS2, L0_xattn_Wk, L0_xattn_bk, L0_xattn_Wq, L0_xattn_bq, L0_xattn_Wv, L0_xattn_bv)
    x = x + _L0_attn_ref(_layernorm(x, axis=-1), L0_attn_W_w, L0_attn_W_b, L0_attn_proj_w, L0_attn_proj_b, L0_attn_ln_g, L0_attn_ln_b, L0_attn_rpb)
    x = x + _L0_ffn_ref(_layernorm(x, axis=-1), L0_ffn_w_gate, L0_ffn_w_up, L0_ffn_w_down)
    return x

_drawn_inputs = setup_inputs


def setup_inputs(seed=0):
    import zlib

    import numpy as np

    out = dict(_drawn_inputs(seed))
    spreads = {'L0_xattn_bk': (0.0, 0.8),
     'L0_xattn_bq': (0.0, 0.397),
     'L0_xattn_bv': (0.0, 0.1),
     'L0_attn_W_b': (0.0, 0.478),
     'L0_attn_proj_b': (0.0, 0.1),
     'L0_attn_ln_g': (1.0, 0.2),
     'L0_attn_ln_b': (0.0, 0.1)}
    factors = {'L0_attn_rpb': 5.445, 'L0_ffn_w_gate': 3.863, 'L0_ffn_w_up': 3.583, 'L0_ffn_w_down': 3.568}
    for name, (base, spread) in spreads.items():
        noise = np.random.default_rng([zlib.crc32(name.encode()), seed]).standard_normal(out[name].shape)
        drawn = base * np.exp(spread * noise) if base else spread * noise
        out[name] = jnp.asarray(drawn.astype(out[name].dtype))
    for name, factor in factors.items():
        out[name] = (out[name] * factor).astype(out[name].dtype)
    return out
```

```python
from contextlib import ExitStack

import numpy as np

import concourse.bass as bass
from concourse import mybir

ALU = mybir.AluOpType
ACT = mybir.ActivationFunctionType
AX = mybir.AxisListType
F32 = mybir.dt.float32
F16 = mybir.dt.float16
I32 = mybir.dt.int32

P = 128
B, SQ, D, H = 32, 64, 256, 16
DH = D // H
LK = 1601
KT = D // P
ROWS = B * SQ
TILES = ROWS // P
PAIRS = H // 2
NT = -(-LK // P)
LAST = LK - (NT - 1) * P
CH = 512
HALF = 2 * CH
NCH = -(-LK // CH)
W_SCALE = 256.0
MASK = 32768.0
ROW_M, ROW_MASK, KROWS = 96, 104, 105
LN_EPS = 1e-5
ROUND = 12582912.0
VW = DH + 1


def chunk(c):
    return c * CH, min((c + 1) * CH, LK)


C_ID, C_HM, C_EXT, C_DM, C_IQ = 0, 128, 130, 131, 139
C_ALL = C_IQ + SQ


def constants():
    c = np.zeros((P, C_ALL), np.float32)
    p = np.arange(P)
    c[:, C_ID:C_ID + P] = np.eye(P)
    for a in range(2):
        c[:, C_HM + a] = (p % 32) // DH == a
    c[ROW_MASK, C_EXT] = MASK
    for j in range(PAIRS):
        c[ROW_M + j, C_DM + j] = -1.0
    c[:, C_IQ:C_IQ + SQ] = np.arange(SQ)
    return c


SCHEDULE = [
    ("ST", 0), ("K", 0), ("OT", 0), ("K", 1),
    ("ST", 1), ("K", 2), ("PV", 0), ("K", 3),
    ("ST", 2), ("K", 4), ("PV", 1), ("K", 5),
    ("ST", 3), ("K", 6), ("K", 7), ("PV", 2), ("CH", 0),
    ("ST", 4), ("Q", 0), ("V", 0), ("PV", 3), ("V", 1), ("CH", 1),
    ("ST", 5), ("V", 2), ("MX", 0), ("MX", 1), ("PV", 4), ("MX", 2),
    ("ST", 6), ("MX", 3), ("MX", 4), ("PV", 5), ("MX", 5), ("V", 3), ("MX", 6),
    ("ST", 7), ("MX", 7), ("MX", 8), ("PV", 6), ("MX", 9), ("MX", 10),
    ("ST", 8), ("MX", 11), ("V", 4), ("MX", 12), ("MX", 13), ("PV", 7), ("MX", 14),
    ("ST", 9), ("MX", 15), ("MX", 16), ("PV", 8), ("MX", 17), ("V", 5), ("MX", 18),
    ("ST", 10), ("MX", 19), ("MX", 20), ("PV", 9), ("MX", 21), ("MX", 22),
    ("ST", 11), ("MX", 23), ("PV", 10), ("MX", 24), ("V", 6), ("MX", 25),
    ("ST", 12), ("PV", 11), ("MT", 0),
    ("PV", 12),
]
UNITS = [x for x in SCHEDULE if x[0] in ("Q", "K", "V", "MX", "MT", "OT")]
PER = {k: sum(x[0] == k for x in SCHEDULE) for k in ("Q", "K", "V", "MX", "MT", "OT", "ST", "PV", "CH")}
RING = 3


def inverse_deviation(dve, ve, sd, r, t, step, sqrt_ready, first):
    dve.wait_ge(sqrt_ready, 1)
    dve.reciprocal(r, sd).then_inc(step, 1)
    dve.wait_ge(step, first + 1)
    dve.tensor_tensor(t, r, r, ALU.mult).then_inc(step, 1)
    dve.wait_ge(step, first + 2)
    dve.tensor_tensor(t, t, ve, ALU.mult).then_inc(step, 1)
    dve.wait_ge(step, first + 3)
    dve.tensor_scalar(t, t, -0.5, 1.5, ALU.mult, ALU.add).then_inc(step, 1)
    dve.wait_ge(step, first + 4)
    dve.tensor_tensor(r, r, t, ALU.mult).then_inc(step, 1)
    dve.wait_ge(step, first + 5)


def cross_attention(nc, sb, ctx, dram):
    def alloc(name, shape, dt):
        return ctx.enter_context(nc.sbuf_tensor(name, shape, dt))

    def psum(name, shape):
        return ctx.enter_context(nc.psum_tensor(name, shape, F32))

    def sem(name):
        return ctx.enter_context(nc.semaphore(name))

    X, CST, STAT = sb["X"], sb["CST"], sb["STAT"]
    XT_HI = alloc("XT_HI", [P, KT, ROWS], F16)
    XT_LO = alloc("XT_LO", [P, KT, ROWS], F16)
    XN = alloc("XN", [P, 2, D], F32)
    MV = alloc("MV", [P, TILES, 2], F32)
    RSTD = alloc("RSTD", [P, TILES], F32)
    VE, SD, VT = alloc("VE", [P, TILES], F32), alloc("SD", [P, TILES], F32), alloc("VT", [P, TILES], F32)
    WQ_HI = alloc("WQ_HI", [P, KT, PAIRS, 4, 32], F16)
    WQ_LO = alloc("WQ_LO", [P, KT, PAIRS, 4, 32], F16)
    WK_HI = alloc("WK_HI", [P, KT, D], F16)
    WK_LO = alloc("WK_LO", [P, KT, D], F16)
    WV_HI = alloc("WV_HI", [P, KT, D], F16)
    WV_LO = alloc("WV_LO", [P, KT, D], F16)
    BQ = alloc("BQ", [P, PAIRS], F32)
    BK = alloc("BK", [P, KT], F32)
    BV = alloc("BV", [P, D], F32)
    LENI = alloc("LENI", [P, B], I32)
    LEN = alloc("LEN", [P, B], F32)
    LENP = alloc("LENP", [B, 1], F32)
    LENPI = alloc("LENPI", [B, 1], I32)
    CTX = alloc("CTX", [P, KT, LK], F32)
    CTX_HI = alloc("CTX_HI", [P, 2, KT, LK], F16)
    CTX_LO = alloc("CTX_LO", [P, 2, KT, LK], F16)
    K_HI = alloc("K_HI", [P, KT, LK], F16)
    K_LO = alloc("K_LO", [P, KT, LK], F16)
    K32 = alloc("K32", [P, 2, CH], F32)
    STK_MEM = [alloc(f"STK{u}", [P, PAIRS * LK], F16) for u in range(2)]
    STK = [mem[:, :].rearrange("p (j t) -> p j t", j=PAIRS) for mem in STK_MEM]
    V = [alloc(f"V{u}", [P, NT, H, VW], F32) for u in range(2)]
    PR = alloc("PR", [P, 2, H * SQ], F32)
    QS = alloc("QS", [P, 2, PAIRS, 2, SQ], F16)
    Q1 = alloc("Q1", [P, PAIRS, SQ], F32)
    Q2 = alloc("Q2", [P, PAIRS, SQ], F32)
    QU = alloc("QU", [P, PAIRS, SQ], F16)
    MXP = alloc("MXP", [P, PAIRS, NCH], F32)
    MCOL = alloc("MCOL", [P, P], F32)
    OSB = alloc("OSB", [P, 4, SQ], F32)
    RDEN = alloc("RDEN", [P, H], F32)
    OTMP = alloc("OTMP", [P, H, DH], F32)

    S_PS = [psum(f"S_PS{i}", [P, H * SQ]) for i in range(2)]
    O_PS = psum("O_PS", [P, 512])
    W_PS = [psum(f"W_PS{i}", [P, 512]) for i in range(RING)]

    V1 = V[1][0:B].rearrange("p t h v -> p (t h v)")
    TOKI = V1[:, 0:LK]
    KMH = V1[:, LK + 1:2 * LK + 1].bitcast(F16)[:, 0:LK]
    PRF = PR[:, :, :].rearrange("p a r -> p (a r)")
    W_RAW = [PRF[:, i * KT * D:(i + 1) * KT * D].rearrange("p (k n) -> p k n", k=KT) for i in range(3)]

    in_x, in_cst, in_wq, in_b, in_tok, in_ctx = (sem(s) for s in ("in_x", "in_cst", "in_wq", "in_b", "in_tok", "in_ctx"))
    in_wk, in_wv = sem("in_wk"), sem("in_wv")
    ln_step, ln_stat, xn_ready, xt_ps, xt_hi, xt_lo = (sem(s) for s in ("ln_step", "ln_stat", "xn_ready", "xt_ps", "xt_hi", "xt_lo"))
    w_step, mask_ready, mask_out, init_done, pool_init = (sem(s) for s in ("w_step", "mask_ready", "mask_out", "init_done", "pool_init"))
    root_ready, wq_spread = sem("root_ready"), sem("wq_spread")
    ctx_hi, ctx_lo = sem("ctx_hi"), sem("ctx_lo")
    k_ps, k_hi, k_32, k_lo = sem("k_ps"), sem("k_hi"), sem("k_32"), sem("k_lo")
    stk_a, stk_b = sem("stk_a"), sem("stk_b")
    v_ps, v_sb = sem("v_ps"), sem("v_sb")
    q_ps, q_step = sem("q_ps"), sem("q_step")
    mx_ps, mx_done, m_col, m_ps, m_rows = (sem(s) for s in ("mx_ps", "mx_done", "m_col", "m_ps", "m_rows"))
    s_ps, p_sb, pv_done, o_sb, o_ps, o_step = (sem(s) for s in ("s_ps", "p_sb", "pv_done", "o_sb", "o_ps", "o_step"))
    QSTEPS, OSTEPS = 7, 4
    A_DMAS, B_DMAS = 13, 12

    def need(eng, s, value):
        if isinstance(value, int) and value <= 0:
            return
        eng.wait_ge(s, value)

    def free_bank(eng, b, pos, skipped):
        n, p = b, pos
        while True:
            p -= RING
            if p < 0:
                n, p = n - 1, max(q for q in range(len(UNITS)) if q % RING == pos % RING)
                if isinstance(n, int) and n < -1:
                    return
            kind, i = UNITS[p]
            if not skipped(kind, n):
                break
        m = n + 1
        if kind == "K":
            need(eng, k_hi, PER["K"] * m + i + 1)
            need(eng, k_32, PER["K"] * m + i + 1)
        elif kind == "V":
            need(eng, v_sb, PER["V"] * m + i + 1)
        elif kind == "Q":
            need(eng, q_step, QSTEPS * m + 1)
        elif kind == "MX":
            need(eng, mx_done, PER["MX"] * m + i + 1)
        elif kind == "MT":
            need(eng, m_rows, m + 1)
        elif kind == "OT":
            need(eng, o_step, OSTEPS * (n - 1) + 2)

    def skip_for(b):
        def skipped(kind, n):
            if isinstance(n, int):
                if kind == "OT":
                    return n < 1
                return n >= B - 1
            return False
        return skipped

    def items(b, attend, prepare, split):
        for kind, i in SCHEDULE:
            if kind in ("ST", "PV") and not attend:
                continue
            if kind in ("Q", "K", "V", "MX", "MT") and not prepare:
                continue
            if kind == "CH" and not split:
                continue
            if kind == "OT" and isinstance(b, int) and b < 1:
                continue
            yield kind, i, (UNITS.index((kind, i)) if (kind, i) in UNITS else None)

    def run(eng, body):
        body(-1, 1, False, True, False)
        body(0, 0, True, True, True)
        body(0, 1, True, True, True)
        with eng.Fori(1, B // 2 - 1) as g:
            body(g, 0, True, True, True)
            body(g, 1, True, True, True)
        body(B // 2 - 1, 0, True, True, False)
        body(B // 2 - 1, 1, True, False, False)

    block = ctx.enter_context(nc.Block())

    @block.sync
    def _(sp):
        for i, (name, landed) in enumerate((("wk_t", in_wk), ("wq_t", in_wq), ("wv_t", in_wv))):
            sp.dma_start(W_RAW[i], dram[name].rearrange("(k p) n -> p k n", p=P)).then_inc(landed, 16)
        sp.dma_start(X[:, :, :], dram["x"].rearrange("(t p) d -> p t d", p=P)).then_inc(in_x, 16)
        sp.dma_start(TOKI, dram["tok"].broadcast_to([B, LK])).then_inc(in_tok, 16)
        sp.dma_start(LENI[:, :], dram["lens"].broadcast_to([P, B])).then_inc(in_b, 16)
        sp.dma_start(LENPI[:, :], dram["lens"].rearrange("a b -> b a")).then_inc(in_b, 16)
        sp.dma_start(BQ[:, :], dram["bq"]).then_inc(in_b, 16)
        sp.dma_start(BK[:, :], dram["bk"]).then_inc(in_b, 16)
        sp.dma_start(BV[:, :], dram["bv"].rearrange("(a d) -> a d", a=1).broadcast_to([P, D])).then_inc(in_b, 16)

        def load(n):
            need(sp, ctx_lo, 2 * n)
            for k in range(KT):
                sp.dma_start(CTX[:, k, :], dram["ctx_t"][bass.ds(n, 1), k * P:(k + 1) * P, :].rearrange("a p t -> p (a t)"))\
                    .then_inc(in_ctx, 16)

        def stack(n, u, half):
            lo, hi = (0, HALF) if half == 0 else (HALF, LK)
            s = stk_a if half == 0 else stk_b
            if half == 0:
                sp.wait_ge(mask_out, 16)
                need(sp, s_ps, NT * (n - 1))
            need(sp, k_lo, PER["K"] * n + 4 * (half + 1))
            if half == 0:
                sp.dma_start(STK[u][ROW_MASK:ROW_MASK + 1, :, :],
                             dram["kmask"][bass.ds(n, 1), :].rearrange("a (o t) -> a o t", o=1).broadcast_to([1, PAIRS, LK]))\
                    .then_inc(s, 16)
            for c in range(4):
                rows = slice(32 * c, 32 * c + 32)
                for q, part in enumerate((K_HI, K_LO, K_HI)):
                    sp.dma_start(STK[u][32 * q:32 * q + 32, c::4, lo:hi], part[rows, :, lo:hi]).then_inc(s, 16)

        load(0)
        sp.dma_start(CST[:, :], dram["cst"]).then_inc(in_cst, 16)
        sp.wait_ge(mask_ready, 1)
        sp.dma_start(dram["kmask"], KMH).then_inc(mask_out, 16)
        load(1)
        sp.wait_ge(pool_init, 5)

        def body(g, u, attend, prepare, split):
            b = 2 * g + u
            if split:
                load(b + 2)
            if prepare:
                stack(b + 1, 1 - u, 0)
                stack(b + 1, 1 - u, 1)

        run(sp, body)

    @block.gpsimd
    def _(pool):
        pool.memset(MCOL[:, :], 0.0).then_inc(pool_init, 1)
        ones = float(np.ones(2, np.float16).view(np.float32)[0])
        for u in range(2):
            pool.wait_ge(pool_init, u + 1)
            pool.memset(STK_MEM[u][ROW_M:ROW_MASK, :].bitcast(F32), ones).then_inc(pool_init, 1)
        pool.wait_ge(pool_init, 3)
        pool.memset(V[0][:, :, :, DH:VW], 1.0).then_inc(pool_init, 1)
        pool.wait_ge(pool_init, 4)
        pool.wait_ge(mask_out, 16)
        pool.memset(V[1][:, :, :, DH:VW], 1.0).then_inc(pool_init, 1)

        def k_low(n, i):
            lo, hi = chunk(i // 2)
            pool.wait_ge(k_hi, PER["K"] * n + i + 1)
            pool.wait_ge(k_32, PER["K"] * n + i + 1)
            if i < 4:
                need(pool, stk_a, 16 * A_DMAS * n)
            else:
                need(pool, stk_b, 16 * B_DMAS * n)
            pool.tensor_tensor(K_LO[:, i % 2, lo:hi], K32[:, i % 2, 0:hi - lo], K_HI[:, i % 2, lo:hi],
                               ALU.subtract).then_inc(k_lo, 1)

        def ctx_low(n, u, half):
            lo, hi = (0, HALF) if half == 0 else (HALF, LK)
            pool.wait_ge(ctx_hi, 2 * n + half + 1)
            pool.tensor_tensor(CTX_LO[:, u, :, lo:hi], CTX[:, :, lo:hi], CTX_HI[:, u, :, lo:hi],
                               ALU.subtract).then_inc(ctx_lo, 1)

        pool.wait_ge(pool_init, 5)
        ctx_low(0, 0, 0)
        ctx_low(0, 0, 1)
        ctx_low(1, 1, 0)
        ctx_low(1, 1, 1)

        def body(g, u, attend, prepare, split):
            b = 2 * g + u
            for kind, i, _ in items(b, attend, prepare, split):
                if kind == "K":
                    k_low(b + 1, i)
                elif kind == "CH":
                    ctx_low(b + 2, u, i)

        run(pool, body)

    @block.tensor
    def _(pe):
        pe.wait_ge(in_cst, 16)
        for t in range(TILES):
            pe.wait_ge(xn_ready, t + 1)
            if t % 2 == 0 and t >= 4:
                pe.wait_ge(xt_lo, t // 2 - 1)
            for k in range(KT):
                last = pe.transpose(W_PS[t // 2 % 2][:, (2 * k + t % 2) * P:(2 * k + t % 2 + 1) * P],
                                    XN[:, t % 2, k * P:(k + 1) * P], CST[:, C_ID:C_ID + P])
            last.then_inc(xt_ps, 1)
        pe.wait_ge(xt_lo, TILES // 2)
        pe.wait_ge(wq_spread, 2)
        pe.wait_ge(w_step, 9)
        pe.wait_ge(init_done, 2)
        pe.wait_ge(pool_init, 5)

        def body(g, u, attend, prepare, split):
            b = 2 * g + u
            n, w = b + 1, 1 - u
            skipped = skip_for(b)
            for kind, i, pos in items(b, attend, prepare, split):
                if pos is not None:
                    if kind == "OT":
                        pe.wait_ge(in_cst, 16)
                    free_bank(pe, b, pos, skipped)
                    bank = W_PS[pos % RING]
                if kind == "ST":
                    par = (u + i) % 2
                    if i == 0:
                        pe.wait_ge(m_rows, b + 1)
                    need(pe, p_sb, NT * b + i - 1)
                    m = P if i < NT - 1 else LAST
                    for j in range(PAIRS):
                        last = pe.matmul(S_PS[par][0:m, j * 2 * SQ:(j + 1) * 2 * SQ],
                                         STK[u][0:KROWS, j, i * P:i * P + m], QS[0:KROWS, u, j, :, :],
                                         start=True, stop=True)
                    last.then_inc(s_ps, 1)
                elif kind == "PV":
                    par = (u + i) % 2
                    m = P if i < NT - 1 else LAST
                    if i == 0:
                        need(pe, o_sb, b)
                    pe.wait_ge(p_sb, NT * b + i + 1)
                    for h in range(H):
                        r = 32 * (h % 4)
                        last = pe.matmul(O_PS[r:r + VW, (h // 4) * SQ:(h // 4 + 1) * SQ],
                                         V[u][0:m, i, h, :], PR[0:m, par, h * SQ:(h + 1) * SQ],
                                         start=(i == 0 and h < 4), stop=(i == NT - 1), skip_group_check=True)
                    last.then_inc(pv_done, 1)
                elif kind == "K":
                    c, m = i // 2, i % 2
                    lo, hi = chunk(c)
                    pe.wait_ge(ctx_lo, 2 * n + (1 if c < 2 else 2))
                    parts = [(WK_HI, CTX_HI), (WK_HI, CTX_LO), (WK_LO, CTX_HI)]
                    for e, (a, c_) in enumerate([(x, k) for x in parts for k in range(KT)]):
                        last = pe.matmul(bank[:, 0:hi - lo], a[0][:, c_, m * P:(m + 1) * P], a[1][:, w, c_, lo:hi],
                                         start=(e == 0), stop=(e == 5))
                    last.then_inc(k_ps, 1)
                elif kind == "V":
                    for s in range(2 if i < 6 else 1):
                        t = 2 * i + s
                        lo, hi = t * P, min((t + 1) * P, LK)
                        parts = [(CTX_HI, WV_HI), (CTX_HI, WV_LO), (CTX_LO, WV_HI)]
                        for e, (a, k) in enumerate([(x, k) for k in range(KT) for x in parts]):
                            last = pe.matmul(bank[0:hi - lo, s * D:(s + 1) * D], a[0][:, w, k, lo:hi], a[1][:, k, :],
                                             start=(e == 0), stop=(e == 5), skip_group_check=True)
                    last.then_inc(v_ps, 1)
                elif kind == "Q":
                    for j in range(PAIRS):
                        parts = [(WQ_HI, XT_HI), (WQ_HI, XT_LO), (WQ_LO, XT_HI)]
                        for e, (a, k) in enumerate([(x, k) for x in parts for k in range(KT)]):
                            last = pe.matmul(bank[:, j * SQ:(j + 1) * SQ], a[0][:, k, j, :, :],
                                             a[1][:, k, bass.ds(n * SQ, SQ)], start=(e == 0), stop=(e == 5),
                                             skip_group_check=True)
                    last.then_inc(q_ps, 1)
                elif kind == "MX":
                    if i == 0:
                        pe.wait_ge(stk_a, 16 * A_DMAS * (n + 1))
                        pe.wait_ge(q_step, QSTEPS * (n + 1))
                    if i == 16:
                        pe.wait_ge(stk_b, 16 * B_DMAS * (n + 1))
                    if i < 24:
                        lo, hi = chunk(i // 8)
                        todo = [(i % 8, 0)]
                    else:
                        lo, hi = chunk(3)
                        todo = [((i - 24) * 4 + s, s) for s in range(4)]
                    for j, s in todo:
                        last = pe.matmul(bank[:, s * LAST:s * LAST + hi - lo], QS[0:KROWS, w, j, :, :],
                                         STK[w][0:KROWS, j, lo:hi], start=True, stop=True, skip_group_check=True)
                    last.then_inc(mx_ps, 1)
                elif kind == "MT":
                    pe.wait_ge(m_col, n + 1)
                    pe.transpose(bank[:, 0:P], MCOL[:, :], CST[:, C_ID:C_ID + P]).then_inc(m_ps, 1)
                elif kind == "OT":
                    pe.wait_ge(o_sb, b)
                    for g in range(4):
                        last = pe.transpose(bank[0:SQ, g * P:(g + 1) * P], OSB[:, g, :], CST[:, C_ID:C_ID + P])
                    last.then_inc(o_ps, 1)

        run(pe, body)
        pe.wait_ge(o_sb, B)
        pe.wait_ge(o_step, OSTEPS * (B - 2) + 2)
        for g in range(4):
            last = pe.transpose(W_PS[0][0:SQ, g * P:(g + 1) * P], OSB[:, g, :], CST[:, C_ID:C_ID + P])
        last.then_inc(o_ps, 1)

    @block.scalar
    def _(act):
        act.wait_ge(ln_stat, 2 * TILES + 1)
        nc.scalar.activation(SD[:, :], VE[:, :], ACT.Sqrt).then_inc(root_ready, 1)
        act.wait_ge(w_step, 6)
        for w in (WQ_HI, WQ_LO):
            rows = w[:, :, :, :, :].rearrange("p k j c n -> p (k j) c n")
            nc.scalar.activation(rows[:, :, 1:4, :], rows[:, :, 0:1, :].broadcast_to([P, KT * PAIRS, 3, 32]), ACT.Copy)\
                .then_inc(wq_spread, 1)
        for v in range(TILES // 2):
            act.wait_ge(xt_ps, 2 * v + 2)
            nc.scalar.activation(XT_HI[:, :, 2 * v * P:(2 * v + 2) * P], W_PS[v % 2][:, :].rearrange("p (k r) -> p k r", k=KT),
                                 ACT.Copy).then_inc(xt_hi, 1)
        act.wait_ge(in_b, 16 * 5)
        act.wait_ge(w_step, 9)
        act.wait_ge(pool_init, 5)

        def o_copy(b):
            act.wait_ge(pv_done, NT * (b + 1))
            need(act, o_ps, b)
            nc.scalar.activation(OSB[:, :, :], O_PS[:, 0:4 * SQ].rearrange("p (g q) -> p g q", g=4), ACT.Copy)\
                .then_inc(o_sb, 1)

        def body(g, u, attend, prepare, split):
            b = 2 * g + u
            n, w = b + 1, 1 - u
            for kind, i, pos in items(b, attend, prepare, split):
                bank = W_PS[pos % RING] if pos is not None else None
                if kind == "ST":
                    par = (u + i) % 2
                    m = P if i < NT - 1 else LAST
                    act.wait_ge(s_ps, NT * b + i + 1)
                    need(act, pv_done, NT * b + i - 1)
                    nc.scalar.activation(PR[0:m, par, :], S_PS[par][0:m, :], ACT.Exp).then_inc(p_sb, 1)
                elif kind == "K":
                    lo, hi = chunk(i // 2)
                    act.wait_ge(k_ps, PER["K"] * n + i + 1)
                    if i < 4:
                        need(act, stk_a, 16 * A_DMAS * n)
                    else:
                        need(act, stk_b, 16 * B_DMAS * n)
                    nc.scalar.activation(K_HI[:, i % 2, lo:hi], bank[:, 0:hi - lo], ACT.Identity,
                                         bias=BK[:, i % 2:i % 2 + 1], scale=1 / W_SCALE).then_inc(k_hi, 1)
                elif kind == "V":
                    act.wait_ge(v_ps, PER["V"] * n + i + 1)
                    need(act, pv_done, NT * (n - 1))
                    t0, t1, m = (2 * i, 2 * i + 2, P) if i < 6 else (12, 13, LAST)
                    nc.scalar.activation(V[w][0:m, t0:t1, :, 0:DH],
                                         bank[0:m, 0:(t1 - t0) * D].rearrange("p (t h d) -> p t h d", t=t1 - t0, h=H),
                                         ACT.Copy, scale=1 / W_SCALE).then_inc(v_sb, 1)
            if attend:
                o_copy(b)

        run(act, body)

    @block.vector
    def _(dve):
        dve.memset(O_PS[:, :], 0.0).then_inc(init_done, 1)

        def split_w(step, raw, hi, lo, landed):
            dve.wait_ge(landed, 16)
            dve.tensor_scalar(raw, raw, W_SCALE, None, ALU.mult).then_inc(w_step, 1)
            dve.wait_ge(w_step, step + 1)
            dve.tensor_copy(hi, raw).then_inc(w_step, 1)
            dve.wait_ge(w_step, step + 2)
            dve.tensor_tensor(lo, raw, hi, ALU.subtract).then_inc(w_step, 1)

        split_w(0, W_RAW[0], WK_HI[:, :, :], WK_LO[:, :, :], in_wk)
        wq = W_RAW[1].rearrange("p k (j n) -> p (k j) n", n=32)
        split_w(3, wq, *(w[:, :, :, 0, :].rearrange("p k j n -> p (k j) n") for w in (WQ_HI, WQ_LO)), in_wq)
        split_w(6, W_RAW[2], WV_HI[:, :, :], WV_LO[:, :, :], in_wv)
        dve.wait_ge(in_x, 16)
        for t in range(TILES):
            dve.bn_stats(STAT[:, t, :], X[:, t, :]).then_inc(ln_stat, 1)
        dve.wait_ge(ln_stat, TILES)
        for t in range(TILES):
            dve.bn_aggr(MV[:, t, :], STAT[:, t, :]).then_inc(ln_stat, 1)
        dve.wait_ge(ln_stat, 2 * TILES)
        dve.tensor_scalar(VE[:, :], MV[:, :, 1], LN_EPS, None, ALU.add).then_inc(ln_stat, 1)

        dve.wait_ge(in_b, 16 * 5)
        dve.tensor_copy(LEN[:, :], LENI[:, :]).then_inc(init_done, 1)
        dve.tensor_scalar(BQ[:, :], BQ[:, :], 0.25, None, ALU.mult).then_inc(ln_step, 1)
        dve.tensor_copy(LENP[:, :], LENPI[:, :]).then_inc(ln_step, 1)
        dve.wait_ge(ln_step, 2)
        dve.wait_ge(in_tok, 16)
        dve.tensor_scalar(KMH, TOKI, LENP[:, 0:1], -MASK, ALU.is_ge, ALU.mult).then_inc(mask_ready, 1)

        def ctx_high(n, u, half):
            lo, hi = (0, HALF) if half == 0 else (HALF, LK)
            dve.wait_ge(in_ctx, 16 * KT * (n + 1))
            need(dve, v_ps, PER["V"] * (n - 1))
            dve.tensor_copy(CTX_HI[:, u, :, lo:hi], CTX[:, :, lo:hi]).then_inc(ctx_hi, 1)

        ctx_high(0, 0, 0)
        ctx_high(0, 0, 1)
        inverse_deviation(dve, VE[:, :], SD[:, :], RSTD[:, :], VT[:, :], ln_stat, root_ready, 2 * TILES + 1)
        for t in range(TILES):
            if t >= 2:
                dve.wait_ge(xt_ps, t - 1)
            dve.tensor_scalar(XN[:, t % 2, :], X[:, t, :], MV[:, t, 0:1], RSTD[:, t:t + 1],
                              ALU.subtract, ALU.mult).then_inc(xn_ready, 1)
            if t % 2:
                cols = slice((t - 1) * P, (t + 1) * P)
                dve.wait_ge(xt_hi, t // 2 + 1)
                dve.tensor_tensor(XT_LO[:, :, cols], W_PS[t // 2 % 2][:, :].rearrange("p (k r) -> p k r", k=KT),
                                  XT_HI[:, :, cols], ALU.subtract).then_inc(xt_lo, 1)
        ctx_high(1, 1, 0)
        ctx_high(1, 1, 1)

        def query_rows(n, w, bank, col):
            q = QSTEPS * n
            dve.wait_ge(q_ps, n + 1)
            if not isinstance(n, int) or n > 0:
                dve.wait_ge(q_step, q)
            dve.scalar_tensor_tensor(Q1[:, :, :], bank[:, :].rearrange("p (j q) -> p j q", j=PAIRS), 0.25 / W_SCALE,
                                     BQ[:, :].unsqueeze(2).broadcast_to([P, PAIRS, SQ]), ALU.mult, ALU.add).then_inc(q_step, 1)
            dve.wait_ge(q_step, q + 1)
            iq = CST[:, C_IQ:C_IQ + SQ].unsqueeze(1).broadcast_to([P, PAIRS, SQ])
            dve.scalar_tensor_tensor(Q2[:, :, :], iq, LEN[:, col], Q1[:, :, :], ALU.is_lt, ALU.mult).then_inc(q_step, 1)
            dve.wait_ge(q_step, q + 2)
            dve.tensor_copy(QU[0:96], Q2[0:96]).then_inc(q_step, 1)
            dve.wait_ge(q_step, q + 3)
            dve.tensor_tensor(QU[64:96], Q2[64:96], QU[64:96], ALU.subtract).then_inc(q_step, 1)
            dve.wait_ge(q_step, q + 4)
            need(dve, s_ps, NT * (n - 1))
            for a in range(2):
                dve.tensor_scalar(QS[0:96, w, :, a, :], QU[0:96], CST[0:96, C_HM + a:C_HM + a + 1], None,
                                  ALU.mult).then_inc(q_step, 1)
            ie = CST[ROW_M:P, C_IQ:C_IQ + SQ].unsqueeze(1).broadcast_to([32, H, SQ])
            dve.tensor_scalar(QS[ROW_M:P, w, :, :, :].rearrange("p j a q -> p (j a) q"), ie, LEN[ROW_M:P, col],
                              CST[ROW_M:P, C_EXT:C_EXT + 1], ALU.is_lt, ALU.mult).then_inc(q_step, 1)

        def part_max(n, i, bank):
            dve.wait_ge(mx_ps, PER["MX"] * n + i + 1)
            if i == 0:
                need(dve, m_col, n)
            if i < 24:
                dve.tensor_reduce(MXP[:, i % 8, i // 8:i // 8 + 1], bank[:, :], AX.X, ALU.max).then_inc(mx_done, 1)
            else:
                g = 4 * (i - 24)
                dve.tensor_reduce(MXP[:, g:g + 4, 3], bank[:, 0:4 * LAST].rearrange("p (j t) -> p j t", j=4),
                                  AX.X, ALU.max).then_inc(mx_done, 1)
            if i == PER["MX"] - 1:
                dve.wait_ge(mx_done, PER["MX"] * (n + 1))
                need(dve, m_ps, n)
                dve.tensor_reduce(MCOL[:, ROW_M:ROW_M + PAIRS], MXP[:, :, :], AX.X, ALU.max).then_inc(m_col, 1)

        def max_rows(n, w, bank):
            dve.wait_ge(m_ps, n + 1)
            rows = slice(ROW_M, ROW_M + PAIRS)
            dve.tensor_tensor(QS[rows, w].rearrange("p j a q -> p j (a q)"),
                              bank[rows, 0:P].unsqueeze(1).broadcast_to([PAIRS, PAIRS, P]),
                              CST[rows, C_DM:C_DM + PAIRS].unsqueeze(2).broadcast_to([PAIRS, PAIRS, P]),
                              ALU.mult).then_inc(m_rows, 1)

        def out_rows(b, u, tile, bank):
            o = OSTEPS * b
            rows = slice(64 * u, 64 * u + 64)
            dve.wait_ge(o_ps, b + 1)
            if not isinstance(b, int) or b > 0:
                dve.wait_ge(o_step, o)
            heads = bank[0:SQ, :].rearrange("p (h d) -> p h d", h=H)
            dve.reciprocal(RDEN[rows, :], heads[:, :, DH]).then_inc(o_step, 1)
            dve.wait_ge(o_step, o + 1)
            dve.tensor_tensor(OTMP[rows], heads[:, :, 0:DH], RDEN[rows, :].unsqueeze(2).broadcast_to([SQ, H, DH]),
                              ALU.mult).then_inc(o_step, 1)
            dve.wait_ge(o_step, o + 2)
            o2 = OTMP[rows].rearrange("p h d -> p (h d)")
            dve.tensor_tensor(o2, o2, BV[rows, :], ALU.add).then_inc(o_step, 1)
            dve.wait_ge(o_step, o + 3)
            xr = X[rows, bass.ds(tile, 1), :].rearrange("p a d -> p (a d)")
            dve.tensor_tensor(xr, xr, o2, ALU.add).then_inc(o_step, 1)

        dve.wait_ge(in_cst, 16)
        dve.wait_ge(init_done, 2)

        def body(g, u, attend, prepare, split):
            b = 2 * g + u
            n, w = b + 1, 1 - u
            for kind, i, pos in items(b, attend, prepare, split):
                bank = W_PS[pos % RING] if pos is not None else None
                if kind == "K":
                    lo, hi = chunk(i // 2)
                    dve.wait_ge(k_hi, PER["K"] * n + i + 1)
                    need(dve, k_lo, PER["K"] * n + i - 1)
                    dve.tensor_scalar(K32[:, i % 2, 0:hi - lo], bank[:, 0:hi - lo], 1 / W_SCALE, BK[:, i % 2:i % 2 + 1],
                                      ALU.mult, ALU.add).then_inc(k_32, 1)
                elif kind == "Q":
                    query_rows(n, w, bank, bass.ds(n, 1))
                elif kind == "MX":
                    part_max(n, i, bank)
                elif kind == "MT":
                    max_rows(n, w, bank)
                elif kind == "OT":
                    out_rows(b - 1, 1 - u, g - 1 + u, bank)
                elif kind == "CH":
                    ctx_high(b + 2, u, i)

        run(dve, body)
        out_rows(B - 1, 1, TILES - 1, W_PS[0])


def deviations(dve, stat, mv, ve, sd, r, t, step, root_ready, base=0):
    for i in range(TILES):
        dve.bn_aggr(mv[:, i, :], stat[:, i, :]).then_inc(step, 1)
    dve.wait_ge(step, base + TILES)
    dve.tensor_scalar(ve, mv[:, :, 1], LN_EPS, None, ALU.add).then_inc(step, 1)
    inverse_deviation(dve, ve, sd, r, t, step, root_ready, base + TILES + 1)


LN_ROOT = TILES + 1
LN_STEPS = TILES + 6


def self_attention(nc, sb, ctx, dram):
    def alloc(name, shape, dt):
        return ctx.enter_context(nc.sbuf_tensor(name, shape, dt))

    def psum(name, shape):
        return ctx.enter_context(nc.psum_tensor(name, shape, F32))

    def sem(name):
        return ctx.enter_context(nc.semaphore(name))

    X, CST, STAT = sb["X"], sb["CST"], sb["STAT"]
    XN = alloc("XN2", [P, TILES, D], F32)
    XHI = alloc("XHI", [P, KT, ROWS], F16)
    XLO = alloc("XLO", [P, KT, ROWS], F16)
    MV = alloc("MV2", [P, TILES, 2], F32)
    VE, SD, RS, VT = (alloc(s, [P, TILES], F32) for s in ("VE2", "SD2", "RS2", "VT2"))
    WRAW = alloc("WRAW2", [P, KT, 3 * D], F32)
    WHI = alloc("WHI2", [P, KT, 3 * D], F16)
    WLO = alloc("WLO2", [P, KT, 3 * D], F16)
    BQK = alloc("BQK", [P, 4], F32)
    BV = alloc("BV2", [P, D], F32)
    BP, LG, LB = (alloc(s, [P, D], F32) for s in ("BP", "LG", "LB"))
    WP = alloc("WP", [P, 4, D], F32)
    BIAS = alloc("BIAS", [P, PAIRS, SQ], F32)
    QK_HI = alloc("QK_HI", [P, 4, ROWS], F16)
    QK_LO = alloc("QK_LO", [P, 4, ROWS], F16)
    QK32 = alloc("QK32", [P, 2, CH], F32)
    V = alloc("V2", [P, TILES, D], F32)
    VS = alloc("VS", [P, 2, 2, D], F32)
    SK = alloc("SK", [96, PAIRS, ROWS], F16)
    SQS = alloc("SQS", [96, PAIRS, ROWS], F16)
    QZ = alloc("QZ", [96, 2, PAIRS, 2, 2, SQ], F16)
    T = alloc("T", [P, 2, PAIRS, 2, SQ], F32)
    MX = alloc("MX2", [P, 2, PAIRS, 2], F32)
    SM = alloc("SM2", [P, 2, PAIRS, 2], F32)
    PT = XHI[:, :, :].rearrange("p k r -> p (k r)").bitcast(F32).rearrange("p (u j r) -> p u j r", u=2, j=PAIRS)
    OT = XLO[:, 0, :].bitcast(F32).rearrange("p (u g r) -> p u g r", u=2, g=4)

    S_PS = [psum(f"S2_PS{i}", [P, 1024]) for i in range(2)]
    T_PS = psum("T2_PS", [P, 1024])
    O_PS = psum("O2_PS", [P, 512])
    Y_PS = psum("Y2_PS", [P, 512])
    RINGS = [S_PS[0][:, 0:512], S_PS[0][:, 512:1024], S_PS[1][:, 0:512], S_PS[1][:, 512:1024]]

    names = ("in_w2 in_small in_wp ln2 root2 tr_ps tr_hi tr_lo w2 qk_ps qk_hi qk_32 qk_lo v2_ps v2_sb stacked "
             "vs bias_ok bp_added zeroed s2_ps qz t_a t_max t_sub t_exp t_sum t_norm p2_ps pt_sb pv2 ot_sb y_ps y_sb "
             "xn2 y_stat x1_stat ln2b root2b y_scaled x2_done b_done").split()
    sm = {s: sem(s) for s in names}
    N_SMALL = 6

    block = ctx.enter_context(nc.Block())

    @block.sync
    def _(sp):
        sp.dma_start(WRAW[:, :, :], dram["w_t"].rearrange("(k p) n -> p k n", p=P)).then_inc(sm["in_w2"], 16)
        sp.dma_start(BQK[:, :], dram["bqk"]).then_inc(sm["in_small"], 16)
        for tile, name in ((BV, "bv2"), (BP, "bp"), (LG, "ln_g"), (LB, "ln_b")):
            sp.dma_start(tile[:, :], dram[name].rearrange("(a d) -> a d", a=1).broadcast_to([P, D])).then_inc(sm["in_small"], 16)
        sp.dma_start(BIAS[:, :, :], dram["bias"]).then_inc(sm["in_small"], 16)
        sp.dma_start(WP[:, :, :], dram["wp"]).then_inc(sm["in_wp"], 16)
        for dst, m0, parts in ((SK, 2, (QK_HI, QK_LO, QK_HI)), (SQS, 0, (QK_HI, QK_HI, QK_LO))):
            units = 8 if m0 == 2 else 16
            sp.wait_ge(sm["qk_hi"], units)
            sp.wait_ge(sm["qk_lo"], units)
            for c in range(4):
                for q, part in enumerate(parts):
                    sp.dma_start(dst[32 * q:32 * q + 32, c::4, :], part[32 * c:32 * c + 32, m0:m0 + 2, :])\
                        .then_inc(sm["stacked"], 16)
        sp.wait_ge(sm["stacked"], 16 * 24)

    def qk_unit(i):
        return (2 if i < 8 else 0) + i % 2, i % 8 // 2 * CH

    def steps(eng, body):
        for s in range(4):
            body(s, s % 2)
        with eng.Fori(2, TILES // 2 - 1) as g:
            body(2 * g, 0)
            body(2 * g + 1, 1)
        for s in range(TILES - 2, TILES + 3):
            body(s, s % 2)

    def live(s, lag):
        return not isinstance(s, int) or 0 <= s - lag < TILES

    def need(eng, s, value):
        if isinstance(value, int) and value <= 0:
            return
        eng.wait_ge(s, value)

    @block.tensor
    def _(pe):
        for t in range(TILES):
            pe.wait_ge(sm["xn2"], t + 1)
            if t % 2 == 0 and t >= 4:
                pe.wait_ge(sm["tr_lo"], t // 2 - 1)
            for k in range(KT):
                last = pe.transpose(RINGS[t // 2 % 2][:, (2 * k + t % 2) * P:(2 * k + t % 2 + 1) * P],
                                    XN[:, t, k * P:(k + 1) * P], CST[:, C_ID:C_ID + P])
            last.then_inc(sm["tr_ps"], 1)
        pe.wait_ge(sm["w2"], 3)
        for i in range(16):
            m, lo = qk_unit(i)
            pe.wait_ge(sm["tr_lo"], 2 * (lo // CH) + 2)
            if i >= 2:
                pe.wait_ge(sm["qk_32"], i - 1)
            parts = [(WHI, XHI), (WHI, XLO), (WLO, XHI)]
            for e, (a, k) in enumerate([(x, k) for x in parts for k in range(KT)]):
                last = pe.matmul(RINGS[2 + i % 2], a[0][:, k, m * P:(m + 1) * P], a[1][:, k, lo:lo + CH],
                                 start=(e == 0), stop=(e == 5))
            last.then_inc(sm["qk_ps"], 1)
        for v in range(TILES // 2):
            if v < 2:
                pe.wait_ge(sm["tr_lo"], TILES // 2)
            else:
                pe.wait_ge(sm["v2_sb"], v - 1)
            for s in range(2):
                lo = (2 * v + s) * P
                parts = [(XHI, WHI), (XHI, WLO), (XLO, WHI)]
                for e, (a, k) in enumerate([(x, k) for k in range(KT) for x in parts]):
                    last = pe.matmul(RINGS[v % 2][:, s * D:(s + 1) * D], a[0][:, k, lo:lo + P], a[1][:, k, 2 * D:3 * D],
                                     start=(e == 0), stop=(e == 5), skip_group_check=True)
            last.then_inc(sm["v2_ps"], 1)
        pe.wait_ge(sm["stacked"], 16 * 24)
        pe.wait_ge(sm["v2_sb"], TILES // 2)
        pe.wait_ge(sm["qk_32"], 16)
        pe.wait_ge(sm["zeroed"], 2)
        pe.wait_ge(sm["in_wp"], 16)

        def body(s, u):
            if live(s, 0):
                pe.wait_ge(sm["qz"], 2 * s + 2)
                need(pe, sm["t_a"], 2 * s - 2)
                for j in range(PAIRS):
                    for w in range(2):
                        last = pe.matmul(S_PS[u][:, (2 * j + w) * SQ:(2 * j + w + 1) * SQ],
                                         QZ[:, u, j, w, :, :],
                                         SK[:, j, bass.ds(s * P + w * SQ, SQ)], start=True, stop=True, skip_group_check=True)
                last.then_inc(sm["s2_ps"], 1)
            if live(s, 2):
                t = s - 2
                pe.wait_ge(sm["pt_sb"], t + 1)
                pe.wait_ge(sm["vs"], 2 * t + 2)
                need(pe, sm["ot_sb"], t)
                for w in range(2):
                    for h in range(H):
                        r = 32 * (h % 4)
                        last = pe.matmul(O_PS[r:r + DH, (h // 4) * P + w * SQ:(h // 4) * P + (w + 1) * SQ],
                                         VS[:, u, w, h * DH:(h + 1) * DH],
                                         PT[:, u, h // 2, (h % 2) * SQ:(h % 2 + 1) * SQ],
                                         start=True, stop=True, skip_group_check=True)
                last.then_inc(sm["pv2"], 1)
            if live(s, 3):
                t = s - 3
                pe.wait_ge(sm["ot_sb"], t + 1)
                need(pe, sm["y_sb"], t)
                for g in range(4):
                    last = pe.matmul(Y_PS[:, 0:D], OT[:, 1 - u, g, :], WP[:, g, :], start=(g == 0), stop=(g == 3))
                last.then_inc(sm["y_ps"], 1)
            if live(s, 1):
                t = s - 1
                pe.wait_ge(sm["t_norm"], t + 1)
                need(pe, sm["pt_sb"], t)
                for j in range(PAIRS):
                    last = pe.transpose(T_PS[:, j * P:(j + 1) * P], T[:, 1 - u, j, :, :].rearrange("p w k -> p (w k)"),
                                        CST[:, C_ID:C_ID + P])
                last.then_inc(sm["p2_ps"], 1)

        steps(pe, body)

    @block.scalar
    def _(act):
        act.wait_ge(sm["ln2"], LN_ROOT)
        nc.scalar.activation(SD[:, :], VE[:, :], ACT.Sqrt).then_inc(sm["root2"], 1)
        for v in range(TILES // 2):
            act.wait_ge(sm["tr_ps"], 2 * v + 2)
            nc.scalar.activation(XHI[:, :, 2 * v * P:(2 * v + 2) * P], RINGS[v % 2].rearrange("p (k r) -> p k r", k=KT),
                                 ACT.Copy).then_inc(sm["tr_hi"], 1)
        act.wait_ge(sm["in_small"], 16 * N_SMALL)
        for i in range(16):
            m, lo = qk_unit(i)
            act.wait_ge(sm["qk_ps"], i + 1)
            nc.scalar.activation(QK_HI[:, m, lo:lo + CH], RINGS[2 + i % 2], ACT.Identity,
                                 bias=BQK[:, m:m + 1], scale=1 / W_SCALE).then_inc(sm["qk_hi"], 1)

        def body(s, u):
            if live(s, 2):
                t = s - 2
                act.wait_ge(sm["p2_ps"], t + 1)
                need(act, sm["pv2"], t - 1)
                nc.scalar.activation(PT[:, u, :, :], T_PS[:, :].rearrange("p (j r) -> p j r", j=PAIRS), ACT.Copy)\
                    .then_inc(sm["pt_sb"], 1)
            if live(s, 2):
                t = s - 2
                act.wait_ge(sm["pv2"], t + 1)
                need(act, sm["y_ps"], t - 1)
                nc.scalar.activation(OT[:, u, :, :], O_PS[:, :].rearrange("p (g r) -> p g r", g=4), ACT.Copy)\
                    .then_inc(sm["ot_sb"], 1)
            if live(s, 0):
                act.wait_ge(sm["t_sub"], s + 1)
                nc.scalar.activation(T[:, u], T[:, u], ACT.Exp).then_inc(sm["t_exp"], 1)

        steps(act, body)
        act.wait_ge(sm["ln2b"], LN_ROOT)
        nc.scalar.activation(SD[:, :], VE[:, :], ACT.Sqrt).then_inc(sm["root2b"], 1)

    @block.gpsimd
    def _(pool):
        pool.wait_ge(sm["in_small"], 16 * N_SMALL)
        for a in range(2):
            b = BIAS[64 * a:64 * a + 64, :, :]
            pool.affine_select(b, b, pattern=[[0, PAIRS], [-1, SQ]], compare_op=ALU.is_ge, fill=-1e30, base=0,
                               channel_multiplier=1).then_inc(sm["bias_ok"], 1)
            pool.wait_ge(sm["bias_ok"], a + 1)
        for i in range(16):
            m, lo = qk_unit(i)
            pool.wait_ge(sm["qk_32"], i + 1)
            pool.tensor_tensor(QK_LO[:, m, lo:lo + CH], QK32[:, i % 2, :], QK_HI[:, m, lo:lo + CH], ALU.subtract)\
                .then_inc(sm["qk_lo"], 1)
        pool.wait_ge(sm["tr_ps"], TILES)
        pool.tensor_tensor(XN[:, :, :], XN[:, :, :], BP[:, :].unsqueeze(1).broadcast_to([P, TILES, D]), ALU.add)\
            .then_inc(sm["bp_added"], 1)

        def body(s, u):
            if live(s, 1):
                t = s - 1
                pool.wait_ge(sm["t_sum"], 2 * t + 2)
                pool.tensor_tensor(T[:, 1 - u], T[:, 1 - u], SM[:, 1 - u].unsqueeze(3).broadcast_to([P, PAIRS, 2, SQ]),
                                   ALU.mult).then_inc(sm["t_norm"], 1)
            if live(s, 0):
                pool.wait_ge(sm["t_max"], s + 1)
                pool.tensor_tensor(T[:, u], T[:, u], MX[:, u].unsqueeze(3).broadcast_to([P, PAIRS, 2, SQ]),
                                   ALU.subtract).then_inc(sm["t_sub"], 1)

        steps(pool, body)
        pool.tensor_tensor(X[:, :, :], X[:, :, :], LB[:, :].unsqueeze(1).broadcast_to([P, TILES, D]), ALU.add)\
            .then_inc(sm["b_done"], 1)

    @block.vector
    def _(dve):
        for i in range(TILES):
            dve.bn_stats(STAT[:, i, :], X[:, i, :]).then_inc(sm["x1_stat"], 1)
        dve.wait_ge(sm["x1_stat"], TILES)
        deviations(dve, STAT, MV, VE[:, :], SD[:, :], RS[:, :], VT[:, :], sm["ln2"], sm["root2"])
        for i in range(TILES):
            dve.tensor_scalar(XN[:, i, :], X[:, i, :], MV[:, i, 0:1], RS[:, i:i + 1], ALU.subtract, ALU.mult)\
                .then_inc(sm["xn2"], 1)
        dve.wait_ge(sm["in_w2"], 16)
        dve.tensor_scalar(WRAW[:, :, :], WRAW[:, :, :], W_SCALE, None, ALU.mult).then_inc(sm["w2"], 1)
        dve.wait_ge(sm["w2"], 1)
        dve.tensor_copy(WHI[:, :, :], WRAW[:, :, :]).then_inc(sm["w2"], 1)
        dve.wait_ge(sm["w2"], 2)
        dve.tensor_tensor(WLO[:, :, :], WRAW[:, :, :], WHI[:, :, :], ALU.subtract).then_inc(sm["w2"], 1)
        for v in range(TILES // 2):
            cols = slice(2 * v * P, (2 * v + 2) * P)
            dve.wait_ge(sm["tr_hi"], v + 1)
            dve.tensor_tensor(XLO[:, :, cols], RINGS[v % 2].rearrange("p (k r) -> p k r", k=KT), XHI[:, :, cols],
                              ALU.subtract).then_inc(sm["tr_lo"], 1)
        dve.memset(O_PS[:, :], 0.0).then_inc(sm["zeroed"], 1)
        dve.memset(VS[:, :, :, :], 0.0).then_inc(sm["zeroed"], 1)
        dve.wait_ge(sm["zeroed"], 2)
        dve.wait_ge(sm["in_small"], 16 * N_SMALL)
        for i in range(16):
            m = qk_unit(i)[0]
            dve.wait_ge(sm["qk_hi"], i + 1)
            if i >= 2:
                dve.wait_ge(sm["qk_lo"], i - 1)
            dve.tensor_scalar(QK32[:, i % 2, :], RINGS[2 + i % 2], 1 / W_SCALE, BQK[:, m:m + 1], ALU.mult, ALU.add)\
                .then_inc(sm["qk_32"], 1)
        for v in range(TILES // 2):
            dve.wait_ge(sm["v2_ps"], v + 1)
            dve.scalar_tensor_tensor(V[:, 2 * v:2 * v + 2, :], RINGS[v % 2].rearrange("p (t d) -> p t d", t=2), 1 / W_SCALE,
                                     BV[:, :].unsqueeze(1).broadcast_to([P, 2, D]), ALU.mult, ALU.add).then_inc(sm["v2_sb"], 1)
        dve.wait_ge(sm["v2_sb"], TILES // 2)
        dve.wait_ge(sm["stacked"], 16 * 24)
        dve.wait_ge(sm["bias_ok"], 2)
        dve.wait_ge(sm["bp_added"], 1)

        def queries(s, u):
            need(dve, sm["s2_ps"], s - 1)
            for a in range(2):
                dve.tensor_scalar(QZ[:, u, :, :, a, :],
                                  SQS[:, :, bass.ds(s * P, P)].rearrange("p j (w q) -> p j w q", w=2),
                                  CST[0:96, C_HM + a:C_HM + a + 1], None, ALU.mult).then_inc(sm["qz"], 1)

        queries(0, 0)

        def body(s, u):
            if live(s, 1):
                t = s - 1
                dve.wait_ge(sm["t_exp"], t + 1)
                need(dve, sm["t_norm"], t - 1)
                dve.tensor_reduce(SM[:, 1 - u], T[:, 1 - u], AX.X, ALU.add).then_inc(sm["t_sum"], 1)
                dve.wait_ge(sm["t_sum"], 2 * t + 1)
                dve.reciprocal(SM[:, 1 - u], SM[:, 1 - u]).then_inc(sm["t_sum"], 1)
            if live(s, 0):
                dve.wait_ge(sm["s2_ps"], s + 1)
                need(dve, sm["p2_ps"], s - 1)
                for w in range(2):
                    dve.scalar_tensor_tensor(T[:, u, :, w, :],
                                             S_PS[u][:, :].rearrange("p (j w k) -> p j w k", j=PAIRS, w=2)[:, :, w, :],
                                             1 / 16, BIAS[:, :, :], ALU.mult, ALU.add).then_inc(sm["t_a"], 1)
                dve.wait_ge(sm["t_a"], 2 * s + 2)
                need(dve, sm["t_sub"], s - 1)
                dve.tensor_reduce(MX[:, u], T[:, u], AX.X, ALU.max).then_inc(sm["t_max"], 1)
            if live(s, -1):
                queries(s + 1, 1 - u)
            if live(s, 1):
                t = s - 1
                need(dve, sm["pv2"], t - 1)
                for w in range(2):
                    rows = slice(64 * w, 64 * w + 64)
                    dve.tensor_copy(VS[rows, 1 - u, w, :], V[rows, bass.ds(t, 1), :].rearrange("p a d -> p (a d)"))\
                        .then_inc(sm["vs"], 1)
            if live(s, 3):
                t = s - 3
                dve.wait_ge(sm["y_ps"], t + 1)
                y = XN[:, bass.ds(t, 1), :].rearrange("p a d -> p (a d)")
                dve.tensor_tensor(y, Y_PS[:, 0:D], y, ALU.add).then_inc(sm["y_sb"], 1)
                dve.wait_ge(sm["y_sb"], t + 1)
                dve.bn_stats(STAT[:, bass.ds(t, 1), :].rearrange("p a s -> p (a s)"), y).then_inc(sm["y_stat"], 1)

        steps(dve, body)
        dve.wait_ge(sm["y_stat"], TILES)
        deviations(dve, STAT, MV, VE[:, :], SD[:, :], RS[:, :], VT[:, :], sm["ln2b"], sm["root2b"])
        dve.wait_ge(sm["b_done"], 1)
        for i in range(TILES + 2):
            if i < TILES:
                dve.scalar_tensor_tensor(XN[:, i, :], XN[:, i, :], MV[:, i, 0:1], LG[:, :], ALU.subtract, ALU.mult)\
                    .then_inc(sm["y_scaled"], 1)
            if 1 <= i <= TILES:
                dve.wait_ge(sm["y_scaled"], i)
                dve.scalar_tensor_tensor(X[:, i - 1, :], XN[:, i - 1, :], RS[:, i - 1:i], X[:, i - 1, :], ALU.mult, ALU.add)\
                    .then_inc(sm["x2_done"], 1)
            if i >= 2:
                dve.wait_ge(sm["x2_done"], i - 1)
                dve.bn_stats(STAT[:, i - 2, :], X[:, i - 2, :]).then_inc(sm["y_stat"], 1)
        dve.wait_ge(sm["y_stat"], 2 * TILES)




INNER = 768
FT = INNER // P
WBLOCK = 32
A_MAX = 32767.0
W_MAX = 7.0
TINY = 1e-12
U16 = 65536.0


def feed_forward(nc, sb, ctx, dram):
    def alloc(name, shape, dt):
        return ctx.enter_context(nc.sbuf_tensor(name, shape, dt))

    def psum(name, shape):
        return ctx.enter_context(nc.psum_tensor(name, shape, F32))

    X, CST = sb["X"], sb["CST"]
    NBLK = INNER * D // P // WBLOCK
    XN = alloc("XN3", [P, TILES, D], F32)
    XT = alloc("XT3", [P, KT, ROWS], F32)
    MV = alloc("MV3", [P, TILES, 2], F32)
    VE, SD, RS, VT = (alloc(s, [P, TILES], F32) for s in ("VE3", "SD3", "RS3", "VT3"))
    WN = alloc("WN", [P, 3, INNER * D // P], F32)
    WS = alloc("WS", [P, 3, NBLK], F32)
    WI = alloc("WI", [P, 3, NBLK], F32)
    WUT = alloc("WUT", [P, KT, INNER], F32)
    WGT = alloc("WGT", [P, KT, INNER], F32)
    WDT = alloc("WDT", [P, FT, D], F32)
    U = alloc("U", [P, FT, ROWS], F32)
    G = alloc("G", [P, FT, ROWS], F32)
    SG = alloc("SG", [P, 2, ROWS], F32)
    AM = alloc("AM", [P, 5, 24], F32)
    AC = alloc("AC", [P, 5], F32)
    A1 = alloc("A1", [1, 5], F32)
    ONE = alloc("ONE", [1, P], F32)
    WORTH = alloc("WORTH", [P, 5], F32)
    SC = alloc("SC", [P, 5], F32)
    INV = alloc("INV", [P, 5], F32)
    RND = alloc("RND", [P, 1], F32)
    W_PS = [psum(f"W3_PS{i}", [P, 512]) for i in range(6)]
    M_PS = psum("M3_PS", [P, 512])
    M2_PS = psum("M4_PS", [P, 512])

    names = ("in_wn ln3 xn3 root3 w_max w_step wt_ps wt_sb const acol am_ps am1 ab_ps sc scale xr xq xt_ps xt_sb "
             "up_ps up_sb ga_ps ga_sb um gm ur ui gr gi sg1 sg2 sg3 g2 g2m g2r o om or_ oi dn_ps dn_sb out3").split()
    sm = {s: ctx.enter_context(nc.semaphore(s)) for s in names}
    in_wn = [ctx.enter_context(nc.semaphore(f"in_wn{i}")) for i in range(3)]
    CHUNKS = FT * ROWS // CH
    WSTEPS = 4
    SSTEPS = 5

    def unit(t, i):
        return t[:, i // 4, i % 4 * CH:(i % 4 + 1) * CH]

    block = ctx.enter_context(nc.Block())
    weights = [(WUT, FT, KT), (WGT, FT, KT), (WDT, KT, FT)]

    def groups(w):
        dst, outs, ins = weights[w]
        return [(k, range(o, min(o + 3, outs))) for k in range(ins) for o in range(0, outs, 3)]

    WT_DONE = [len(groups(0)), len(groups(0)) + len(groups(1)), sum(len(groups(w)) for w in range(3))]

    @block.sync
    def _(sp):
        for w, name in enumerate(("w_up", "w_gate", "w_down")):
            f = (FT, FT, KT)[w]
            sp.dma_start(WN[:, w, :].rearrange("p (f d) -> p f d", f=f), dram[name].rearrange("(f p) d -> p f d", p=P))\
                .then_inc(in_wn[w], 16)
        for i in range(TILES // 4):
            sp.wait_ge(sm["dn_sb"], 4 * i + 4)
            sp.dma_start(dram["out"][4 * i * P:(4 * i + 4) * P, :].rearrange("(t p) d -> p t d", p=P), X[:, 4 * i:4 * i + 4, :])\
                .then_inc(sm["out3"], 16)
        sp.wait_ge(sm["out3"], 16 * (TILES // 4))

    @block.gpsimd
    def _(pool):
        for w in range(3):
            blk = WN[:, w, :].rearrange("p (b e) -> p b e", e=WBLOCK)
            n = WSTEPS * w
            pool.wait_ge(sm["w_max"], 3 * w + 3)

            def wide(t):
                return t[:, w, :].unsqueeze(2).broadcast_to([P, NBLK, WBLOCK])

            pool.tensor_tensor(blk, blk, wide(WI), ALU.mult).then_inc(sm["w_step"], 1)
            pool.wait_ge(sm["w_step"], n + 1)
            pool.tensor_scalar(blk, blk, ROUND, ROUND, ALU.add, ALU.subtract).then_inc(sm["w_step"], 1)
            pool.wait_ge(sm["w_step"], n + 2)
            pool.tensor_scalar(blk, blk, -W_MAX - 1, W_MAX, ALU.max, ALU.min).then_inc(sm["w_step"], 1)
            pool.wait_ge(sm["w_step"], n + 3)
            pool.tensor_tensor(blk, blk, wide(WS), ALU.mult).then_inc(sm["w_step"], 1)
        for f in range(FT):
            pool.wait_ge(sm["sg3"], f + 1)
            pool.tensor_tensor(G[:, f, :], G[:, f, :], SG[:, f % 2, :], ALU.mult).then_inc(sm["g2"], 1)

    @block.tensor
    def _(pe):
        count = [0]

        def turn_weight(w):
            dst, outs, ins = weights[w]
            pe.wait_ge(sm["w_step"], WSTEPS * (w + 1))
            for k, os in groups(w):
                n = count[0]
                if n >= 2:
                    pe.wait_ge(sm["wt_sb"], n - 1)
                for e, o in enumerate(os):
                    last = pe.transpose(W_PS[n % 2][:, e * P:(e + 1) * P],
                                        WN[:, w, (o * ins + k) * P:(o * ins + k + 1) * P], CST[:, C_ID:C_ID + P])
                last.then_inc(sm["wt_ps"], 1)
                count[0] += 1

        def spread(q):
            pe.wait_ge(sm["acol"], q + 1)
            pe.transpose(M_PS[0:1, 0:P], AC[:, q:q + 1], CST[:, C_ID:C_ID + P]).then_inc(sm["am_ps"], 1)
            pe.wait_ge(sm["am1"], q + 1)
            if q:
                pe.wait_ge(sm["sc"], SSTEPS * (q - 1) + 1)
            pe.matmul(M2_PS[:, 0:1], ONE[:, :], A1[0:1, q:q + 1], start=True, stop=True).then_inc(sm["ab_ps"], 1)

        pe.wait_ge(sm["const"], 3)
        spread(0)
        for t in range(TILES):
            pe.wait_ge(sm["xq"], t + 1)
            if t % 2 == 0 and t >= 4:
                pe.wait_ge(sm["xt_sb"], t // 2 - 1)
            for k in range(KT):
                last = pe.transpose(W_PS[2 + t // 2 % 2][:, (2 * k + t % 2) * P:(2 * k + t % 2 + 1) * P],
                                    XN[:, t, k * P:(k + 1) * P], CST[:, C_ID:C_ID + P])
            last.then_inc(sm["xt_ps"], 1)

        def inner(w, wt, ps, sbuf, i):
            f, c = i // 4, i % 4
            for k in range(KT):
                last = pe.matmul(W_PS[i % 6][:, :], wt[:, k, f * P:(f + 1) * P], XT[:, k, c * CH:(c + 1) * CH],
                                 start=(k == 0), stop=(k == KT - 1))
            last.then_inc(ps, 1)

        turn_weight(0)
        turn_weight(1)
        pe.wait_ge(sm["wt_sb"], WT_DONE[1])
        for i in range(CHUNKS):
            pe.wait_ge(sm["xt_sb"], 2 * (i % 4) + 2 if i < 4 else TILES // 2)
            if i == 2:
                pe.wait_ge(sm["xt_sb"], TILES // 2)
            if i >= 6:
                pe.wait_ge(sm["up_sb"], i - 5)
            inner(0, WUT, sm["up_ps"], sm["up_sb"], i)
        for i in range(CHUNKS):
            if i < 6:
                pe.wait_ge(sm["up_sb"], CHUNKS - 5 + i)
            else:
                pe.wait_ge(sm["ga_sb"], i - 5)
            inner(1, WGT, sm["ga_ps"], sm["ga_sb"], i)
            if i == CHUNKS // 2:
                spread(1)
        pe.wait_ge(sm["ga_sb"], CHUNKS)
        spread(2)
        turn_weight(2)
        spread(3)
        spread(4)
        pe.wait_ge(sm["wt_sb"], WT_DONE[2])
        for t in range(TILES):
            pe.wait_ge(sm["oi"], t // 4 + 1)
            if t >= 6:
                pe.wait_ge(sm["dn_sb"], t - 5)
            for f in range(FT):
                last = pe.matmul(W_PS[t % 6][:, 0:D], G[:, f, t * P:(t + 1) * P], WDT[:, f, :],
                                 start=(f == 0), stop=(f == FT - 1))
            last.then_inc(sm["dn_ps"], 1)

    @block.scalar
    def _(act):
        count = [0]

        def keep_weight(w):
            dst, outs, ins = weights[w]
            for k, os in groups(w):
                n = count[0]
                act.wait_ge(sm["wt_ps"], n + 1)
                nc.scalar.activation(dst[:, k, os[0] * P:(os[-1] + 1) * P], W_PS[n % 2][:, 0:len(os) * P], ACT.Copy)\
                    .then_inc(sm["wt_sb"], 1)
                count[0] += 1

        act.wait_ge(sm["ln3"], LN_ROOT)
        nc.scalar.activation(SD[:, :], VE[:, :], ACT.Sqrt).then_inc(sm["root3"], 1)
        act.wait_ge(sm["const"], 3)
        keep_weight(0)
        keep_weight(1)
        for t, ps, done in ((U, "up_ps", "up_sb"), (G, "ga_ps", "ga_sb")):
            for i in range(CHUNKS):
                act.wait_ge(sm[ps], i + 1)
                nc.scalar.activation(unit(t, i), W_PS[i % 6][:, :], ACT.Copy).then_inc(sm[done], 1)
        act.wait_ge(sm["gm"], CHUNKS)
        act.wait_ge(sm["scale"], 3)
        for f in range(FT):
            nc.scalar.activation(G[:, f, :], G[:, f, :], ACT.Identity, bias=RND[:, :], scale=INV[:, 2:3]).then_inc(sm["gr"], 1)
        for f in range(FT):
            act.wait_ge(sm["gi"], f + 1)
            if f >= 2:
                act.wait_ge(sm["g2"], f - 1)
            nc.scalar.activation(SG[:, f % 2, :], G[:, f, :], ACT.Sigmoid, scale=SC[:, 2:3]).then_inc(sm["sg1"], 1)
        keep_weight(2)
        act.wait_ge(sm["g2m"], FT)
        act.wait_ge(sm["scale"], 4)
        for f in range(FT):
            nc.scalar.activation(G[:, f, :], G[:, f, :], ACT.Identity, bias=RND[:, :], scale=INV[:, 3:4]).then_inc(sm["g2r"], 1)
        act.wait_ge(sm["om"], FT)
        act.wait_ge(sm["scale"], 5)
        for c in range(4):
            cols = slice(c * CH, (c + 1) * CH)
            nc.scalar.activation(G[:, :, cols], G[:, :, cols], ACT.Identity, bias=RND[:, :], scale=INV[:, 4:5])\
                .then_inc(sm["or_"], 1)

    @block.vector
    def _(dve):
        dve.memset(ONE[:, :], 1.0).then_inc(sm["const"], 1)
        dve.memset(RND[:, :], ROUND).then_inc(sm["const"], 1)
        dve.memset(WORTH[:, 0:1], 1.0).then_inc(sm["const"], 1)
        deviations(dve, sb["STAT"], MV, VE[:, :], SD[:, :], RS[:, :], VT[:, :], sm["ln3"], sm["root3"])
        for w in range(3):
            dve.wait_ge(in_wn[w], 16)
            dve.tensor_reduce(WS[:, w, :], WN[:, w, :].rearrange("p (b e) -> p b e", e=WBLOCK), AX.X, ALU.max,
                              apply_absolute_value=True).then_inc(sm["w_max"], 1)
            dve.wait_ge(sm["w_max"], 3 * w + 1)
            dve.tensor_scalar(WS[:, w, :], WS[:, w, :], 1 / W_MAX, TINY, ALU.mult, ALU.max).then_inc(sm["w_max"], 1)
            dve.wait_ge(sm["w_max"], 3 * w + 2)
            dve.reciprocal(WI[:, w, :], WS[:, w, :]).then_inc(sm["w_max"], 1)
        for i in range(TILES):
            dve.tensor_scalar(XN[:, i, :], X[:, i, :], MV[:, i, 0:1], RS[:, i:i + 1], ALU.subtract, ALU.mult)\
                .then_inc(sm["xn3"], 1)
        dve.wait_ge(sm["xn3"], TILES)
        dve.tensor_reduce(AC[:, 0:1], XN[:, :, :].rearrange("p t d -> p (t d)"), AX.X, ALU.max,
                          apply_absolute_value=True).then_inc(sm["acol"], 1)

        def scales(q, worth=None):
            n = SSTEPS * q
            if worth is not None:
                worth(WORTH[:, q:q + 1]).then_inc(sm["const"], 1)
            dve.wait_ge(sm["const"], 3 + q)
            dve.wait_ge(sm["am_ps"], q + 1)
            dve.tensor_reduce(A1[0:1, q:q + 1], M_PS[0:1, 0:P], AX.X, ALU.max).then_inc(sm["am1"], 1)
            dve.wait_ge(sm["ab_ps"], q + 1)
            col = slice(q, q + 1)
            dve.tensor_scalar(SC[:, col], M2_PS[:, 0:1], WORTH[:, col], None, ALU.mult).then_inc(sm["sc"], 1)
            dve.wait_ge(sm["sc"], n + 1)
            dve.tensor_scalar(SC[:, col], SC[:, col], 1 / A_MAX, TINY, ALU.mult, ALU.max).then_inc(sm["sc"], 1)
            dve.wait_ge(sm["sc"], n + 2)
            dve.reciprocal(INV[:, col], SC[:, col]).then_inc(sm["sc"], 1)
            dve.wait_ge(sm["sc"], n + 3)
            dve.tensor_tensor(INV[:, col], INV[:, col], WORTH[:, col], ALU.mult).then_inc(sm["sc"], 2)
            dve.wait_ge(sm["sc"], n + 5)
            dve.tensor_copy(A1[0:1, col], A1[0:1, col]).then_inc(sm["scale"], 1)

        scales(0)
        for t in range(TILES):
            dve.tensor_scalar(XN[:, t, :], XN[:, t, :], INV[:, 0:1], ROUND, ALU.mult, ALU.add).then_inc(sm["xr"], 1)
            if t:
                dve.wait_ge(sm["xr"], t)
                dve.tensor_scalar(XN[:, t - 1, :], XN[:, t - 1, :], ROUND, None, ALU.subtract).then_inc(sm["xq"], 1)
        dve.wait_ge(sm["xr"], TILES)
        dve.tensor_scalar(XN[:, TILES - 1, :], XN[:, TILES - 1, :], ROUND, None, ALU.subtract).then_inc(sm["xq"], 1)
        for v in range(TILES // 2):
            dve.wait_ge(sm["xt_ps"], 2 * v + 2)
            dve.tensor_copy(XT[:, :, 2 * v * P:(2 * v + 2) * P], W_PS[2 + v % 2][:, :].rearrange("p (k r) -> p k r", k=KT))\
                .then_inc(sm["xt_sb"], 1)

        def maxima(src, q, done, landed):
            for i in range(CHUNKS):
                dve.wait_ge(landed, i + 1)
                dve.tensor_reduce(AM[:, q, i:i + 1], unit(src, i), AX.X, ALU.max, apply_absolute_value=True).then_inc(done, 1)
            dve.wait_ge(done, CHUNKS)
            dve.tensor_reduce(AC[:, q:q + 1], AM[:, q, 0:CHUNKS], AX.X, ALU.max).then_inc(sm["acol"], 1)

        def worth_of_input(out):
            return dve.tensor_copy(out, SC[:, 0:1])

        maxima(U, 1, sm["um"], sm["up_sb"])
        scales(1, worth_of_input)
        for f in range(FT):
            dve.tensor_scalar(U[:, f, :], U[:, f, :], INV[:, 1:2], ROUND, ALU.mult, ALU.add).then_inc(sm["ur"], 1)
        for f in range(FT):
            dve.wait_ge(sm["ur"], f + 1)
            dve.tensor_scalar(U[:, f, :], U[:, f, :], ROUND, None, ALU.subtract).then_inc(sm["ui"], 1)
        maxima(G, 2, sm["gm"], sm["ga_sb"])
        scales(2, worth_of_input)
        for f in range(FT):
            dve.wait_ge(sm["gr"], f + 1)
            dve.tensor_scalar(G[:, f, :], G[:, f, :], ROUND, None, ALU.subtract).then_inc(sm["gi"], 1)

        def gate_max(f):
            dve.wait_ge(sm["g2"], f + 1)
            dve.tensor_reduce(AM[:, 3, f:f + 1], G[:, f, :], AX.X, ALU.max, apply_absolute_value=True).then_inc(sm["g2m"], 1)

        for f in range(FT):
            s = SG[:, f % 2, :]
            dve.wait_ge(sm["sg1"], f + 1)
            dve.tensor_scalar(s, s, U16, U16 - 1, ALU.mult, ALU.min).then_inc(sm["sg2"], 1)
            dve.wait_ge(sm["sg2"], f + 1)
            dve.tensor_scalar(s, s, ROUND, ROUND, ALU.add, ALU.subtract).then_inc(sm["sg3"], 1)
            if f:
                gate_max(f - 1)
        gate_max(FT - 1)
        dve.wait_ge(sm["g2m"], FT)
        dve.tensor_reduce(AC[:, 3:4], AM[:, 3, 0:FT], AX.X, ALU.max).then_inc(sm["acol"], 1)
        scales(3, lambda out: dve.tensor_scalar(out, SC[:, 2:3], 1 / U16, None, ALU.mult))
        for f in range(FT):
            dve.wait_ge(sm["g2r"], f + 1)
            dve.scalar_tensor_tensor(G[:, f, :], G[:, f, :], ROUND, U[:, f, :], ALU.subtract, ALU.mult).then_inc(sm["o"], 1)
            if f:
                dve.wait_ge(sm["o"], f)
                dve.tensor_reduce(AM[:, 4, f - 1:f], G[:, f - 1, :], AX.X, ALU.max, apply_absolute_value=True).then_inc(sm["om"], 1)
        dve.wait_ge(sm["o"], FT)
        dve.tensor_reduce(AM[:, 4, FT - 1:FT], G[:, FT - 1, :], AX.X, ALU.max, apply_absolute_value=True).then_inc(sm["om"], 1)
        dve.wait_ge(sm["om"], FT)
        dve.tensor_reduce(AC[:, 4:5], AM[:, 4, 0:FT], AX.X, ALU.max).then_inc(sm["acol"], 1)
        scales(4, lambda out: dve.tensor_tensor(out, SC[:, 3:4], SC[:, 1:2], ALU.mult))
        for c in range(4):
            cols = slice(c * CH, (c + 1) * CH)
            dve.wait_ge(sm["or_"], c + 1)
            dve.tensor_scalar(G[:, :, cols], G[:, :, cols], ROUND, None, ALU.subtract).then_inc(sm["oi"], 1)
        for t in range(TILES):
            dve.wait_ge(sm["dn_ps"], t + 1)
            dve.scalar_tensor_tensor(X[:, t, :], W_PS[t % 6][:, 0:D], SC[:, 4:5], X[:, t, :], ALU.mult, ALU.add)\
                .then_inc(sm["dn_sb"], 1)


def program(nc, out, **dram):
    with ExitStack() as top:
        kmask = nc.dram_tensor("kmask", (B, LK), F16).ap()
        sb = {"X": top.enter_context(nc.sbuf_tensor("X", [P, TILES, D], F32)),
              "CST": top.enter_context(nc.sbuf_tensor("CST", [P, C_ALL], F32)),
              "STAT": top.enter_context(nc.sbuf_tensor("STAT", [P, TILES, 6], F32))}
        dram = dict(dram, kmask=kmask, out=out)
        with ExitStack() as ctx:
            cross_attention(nc, sb, ctx, dram)
        with ExitStack() as ctx:
            self_attention(nc, sb, ctx, dram)
        with ExitStack() as ctx:
            feed_forward(nc, sb, ctx, dram)


def projection_rows(w):
    rows = np.zeros((4, 32, 4, D), w.dtype)
    rows[:, :DH] = w.T.reshape(4, 4, DH, D).transpose(1, 2, 0, 3)
    return rows.reshape(P, 4, D)


def position_bias(rpb):
    index = np.arange(SQ)[None, :] - np.arange(SQ)[:, None] + SQ - 1
    return np.ascontiguousarray(rpb[index].reshape(SQ, SQ, PAIRS, 2).transpose(3, 0, 2, 1).reshape(P, PAIRS, SQ))


def arrays_of(inp):
    c = np.ascontiguousarray
    return dict(
        x=c(np.asarray(inp["x"]).reshape(ROWS, D)),
        ctx_t=c(np.asarray(inp["ctx_1024"]).transpose(0, 2, 1)),
        lens=c(np.asarray(inp["_lenS2"]).reshape(1, B)),
        wk_t=c(np.asarray(inp["L0_xattn_Wk"]).T), bk=c(np.asarray(inp["L0_xattn_bk"]).reshape(KT, P).T),
        wq_t=c(np.asarray(inp["L0_xattn_Wq"]).T), bq=c(np.tile(np.asarray(inp["L0_xattn_bq"]).reshape(PAIRS, 32).T, (4, 1))),
        wv_t=c(np.asarray(inp["L0_xattn_Wv"]).T), bv=c(inp["L0_xattn_bv"]),
        w_t=c(np.asarray(inp["L0_attn_W_w"]).T),
        bqk=c(np.asarray(inp["L0_attn_W_b"])[:2 * D].reshape(4, P).T), bv2=c(np.asarray(inp["L0_attn_W_b"])[2 * D:]),
        bp=c(inp["L0_attn_proj_b"]), ln_g=c(inp["L0_attn_ln_g"]), ln_b=c(inp["L0_attn_ln_b"]),
        wp=projection_rows(np.asarray(inp["L0_attn_proj_w"])), bias=position_bias(np.asarray(inp["L0_attn_rpb"])),
        w_up=c(inp["L0_ffn_w_up"]), w_gate=c(inp["L0_ffn_w_gate"]), w_down=c(inp["L0_ffn_w_down"]),
        cst=constants(), tok=np.arange(LK, dtype=np.float32).reshape(1, LK))


_OUT = (B, SQ, D)


def kernel(**inputs):
    import concourse.bacc as _bacc
    from concourse.bass_utils import run_bass_kernel_spmd as _run

    nc = _bacc.Bacc("TRN2", target_bir_lowering=False, num_devices=1)
    arrays, aps = {}, {}
    for name, a in arrays_of(inputs).items():
        arrays[f"in_{name}"] = a
        aps[name] = nc.dram_tensor(f"in_{name}", a.shape, mybir.dt.from_np(a.dtype), kind="ExternalInput").ap()
    out = nc.dram_tensor("out", (ROWS, D), F32, kind="ExternalOutput").ap()
    program(nc, out=out, **aps)
    r = _run(nc, [arrays], core_ids=[0])
    return r.results[0]["out"].reshape(_OUT)
```

```python
from contextlib import ExitStack

import numpy as np

import concourse.bass as bass
from concourse import mybir

ALU = mybir.AluOpType
ACT = mybir.ActivationFunctionType
AX = mybir.AxisListType
F32 = mybir.dt.float32
F16 = mybir.dt.float16
I32 = mybir.dt.int32

P = 128
B, SQ, D, H = 32, 64, 256, 16
DH = D // H
LK = 1601
KT = D // P
ROWS = B * SQ
TILES = ROWS // P
PAIRS = H // 2
NT = -(-LK // P)
LAST = LK - (NT - 1) * P
CH = 512
HALF = 2 * CH
NCH = -(-LK // CH)
W_SCALE = 256.0
MASK = 32768.0
ROW_M, ROW_MASK, KROWS = 96, 104, 105
LN_EPS = 1e-5
ROUND = 12582912.0
VW = DH + 1


def chunk(c):
    return c * CH, min((c + 1) * CH, LK)


C_ID, C_HM, C_EXT, C_DM, C_IQ = 0, 128, 130, 131, 139
C_ALL = C_IQ + SQ


def constants():
    c = np.zeros((P, C_ALL), np.float32)
    p = np.arange(P)
    c[:, C_ID:C_ID + P] = np.eye(P)
    for a in range(2):
        c[:, C_HM + a] = (p % 32) // DH == a
    c[ROW_MASK, C_EXT] = MASK
    for j in range(PAIRS):
        c[ROW_M + j, C_DM + j] = -1.0
    c[:, C_IQ:C_IQ + SQ] = np.arange(SQ)
    return c


SCHEDULE = [
    ("ST", 0), ("K", 0), ("OT", 0), ("K", 1),
    ("ST", 1), ("K", 2), ("PV", 0), ("K", 3),
    ("ST", 2), ("K", 4), ("PV", 1), ("K", 5),
    ("ST", 3), ("K", 6), ("K", 7), ("PV", 2), ("CH", 0),
    ("ST", 4), ("Q", 0), ("V", 0), ("PV", 3), ("V", 1), ("CH", 1),
    ("ST", 5), ("V", 2), ("PV", 4), ("MX", 0), ("MX", 1), ("MX", 2),
    ("ST", 6), ("MX", 3), ("MX", 4), ("PV", 5), ("MX", 5), ("V", 3), ("MX", 6),
    ("ST", 7), ("MX", 7), ("MX", 8), ("PV", 6), ("MX", 9), ("MX", 10),
    ("ST", 8), ("MX", 11), ("V", 4), ("MX", 12), ("MX", 13), ("PV", 7), ("MX", 14),
    ("ST", 9), ("MX", 15), ("MX", 16), ("PV", 8), ("MX", 17), ("V", 5), ("MX", 18),
    ("ST", 10), ("MX", 19), ("MX", 20), ("PV", 9), ("MX", 21), ("MX", 22),
    ("ST", 11), ("MX", 23), ("PV", 10), ("MX", 24), ("V", 6), ("MX", 25),
    ("ST", 12), ("PV", 11), ("MT", 0),
    ("PV", 12),
]
UNITS = [x for x in SCHEDULE if x[0] in ("Q", "K", "V", "MX", "MT", "OT")]
PER = {k: sum(x[0] == k for x in SCHEDULE) for k in ("Q", "K", "V", "MX", "MT", "OT", "ST", "PV", "CH")}
RING = 3


def inverse_deviation(dve, ve, sd, r, t, step, sqrt_ready, first):
    dve.wait_ge(sqrt_ready, 1)
    dve.reciprocal(r, sd).then_inc(step, 1)
    dve.wait_ge(step, first + 1)
    dve.tensor_tensor(t, r, r, ALU.mult).then_inc(step, 1)
    dve.wait_ge(step, first + 2)
    dve.tensor_tensor(t, t, ve, ALU.mult).then_inc(step, 1)
    dve.wait_ge(step, first + 3)
    dve.tensor_scalar(t, t, -0.5, 1.5, ALU.mult, ALU.add).then_inc(step, 1)
    dve.wait_ge(step, first + 4)
    dve.tensor_tensor(r, r, t, ALU.mult).then_inc(step, 1)
    dve.wait_ge(step, first + 5)


def cross_attention(nc, sb, ctx, dram):
    def alloc(name, shape, dt):
        return ctx.enter_context(nc.sbuf_tensor(name, shape, dt))

    def psum(name, shape):
        return ctx.enter_context(nc.psum_tensor(name, shape, F32))

    def sem(name):
        return ctx.enter_context(nc.semaphore(name))

    X, CST, STAT = sb["X"], sb["CST"], sb["STAT"]
    XT_HI = alloc("XT_HI", [P, KT, ROWS], F16)
    XT_LO = alloc("XT_LO", [P, KT, ROWS], F16)
    XN = alloc("XN", [P, 4, D], F32)
    MV = alloc("MV", [P, TILES, 2], F32)
    RSTD = alloc("RSTD", [P, TILES], F32)
    VE, SD, VT = alloc("VE", [P, TILES], F32), alloc("SD", [P, TILES], F32), alloc("VT", [P, TILES], F32)
    WQ_HI = alloc("WQ_HI", [P, KT, PAIRS, 4, 32], F16)
    WQ_LO = alloc("WQ_LO", [P, KT, PAIRS, 4, 32], F16)
    WK_HI = alloc("WK_HI", [P, KT, D], F16)
    WK_LO = alloc("WK_LO", [P, KT, D], F16)
    WV_HI = alloc("WV_HI", [P, KT, D], F16)
    WV_LO = alloc("WV_LO", [P, KT, D], F16)
    BQ = alloc("BQ", [P, PAIRS], F32)
    BK = alloc("BK", [P, KT], F32)
    BV = alloc("BV", [P, D], F32)
    LENI = alloc("LENI", [P, B], I32)
    LEN = alloc("LEN", [P, B], F32)
    LENP = alloc("LENP", [B, 1], F32)
    LENPI = alloc("LENPI", [B, 1], I32)
    CTX = alloc("CTX", [P, KT, LK], F32)
    CTX_HI = alloc("CTX_HI", [P, 2, KT, LK], F16)
    CTX_LO = alloc("CTX_LO", [P, 2, KT, LK], F16)
    K_HI = alloc("K_HI", [P, KT, LK], F16)
    K_LO = alloc("K_LO", [P, KT, LK], F16)
    K32 = alloc("K32", [P, 2, CH], F32)
    STK_MEM = [alloc(f"STK{u}", [P, PAIRS * LK], F16) for u in range(2)]
    STK = [mem[:, :].rearrange("p (j t) -> p j t", j=PAIRS) for mem in STK_MEM]
    V = [alloc(f"V{u}", [P, NT, H, VW], F32) for u in range(2)]
    PR = alloc("PR", [P, 2, H * SQ], F32)
    QS = alloc("QS", [P, 2, PAIRS, 2, SQ], F16)
    Q1 = alloc("Q1", [P, PAIRS, SQ], F32)
    Q2 = alloc("Q2", [P, PAIRS, SQ], F32)
    QU = alloc("QU", [P, PAIRS, SQ], F16)
    MXP = alloc("MXP", [P, PAIRS, NCH], F32)
    MCOL = alloc("MCOL", [P, P], F32)
    OSB = alloc("OSB", [P, 4, SQ], F32)
    RDEN = alloc("RDEN", [P, H], F32)
    OTMP = alloc("OTMP", [P, H, DH], F32)

    S_PS = [psum(f"S_PS{i}", [P, H * SQ]) for i in range(2)]
    O_PS = psum("O_PS", [P, 512])
    W_PS = [psum(f"W_PS{i}", [P, 512]) for i in range(RING)]

    V1 = V[1][0:B].rearrange("p t h v -> p (t h v)")
    TOKI = V1[:, 0:LK]
    KMH = V1[:, LK + 1:2 * LK + 1].bitcast(F16)[:, 0:LK]
    PRF = PR[:, :, :].rearrange("p a r -> p (a r)")
    W_RAW = [PRF[:, i * KT * D:(i + 1) * KT * D].rearrange("p (k n) -> p k n", k=KT) for i in range(3)]

    in_x, in_cst, in_wq, in_b, in_tok, in_ctx = (sem(s) for s in ("in_x", "in_cst", "in_wq", "in_b", "in_tok", "in_ctx"))
    in_wk, in_wv = sem("in_wk"), sem("in_wv")
    ln_step, ln_stat, xn_ready, xt_ps, xt_hi, xt_lo = (sem(s) for s in ("ln_step", "ln_stat", "xn_ready", "xt_ps", "xt_hi", "xt_lo"))
    w_step, mask_ready, mask_out, init_done, pool_init = (sem(s) for s in ("w_step", "mask_ready", "mask_out", "init_done", "pool_init"))
    root_ready, wq_spread = sem("root_ready"), sem("wq_spread")
    ctx_hi, ctx_lo = sem("ctx_hi"), sem("ctx_lo")
    k_ps, k_hi, k_32, k_lo = sem("k_ps"), sem("k_hi"), sem("k_32"), sem("k_lo")
    stk_a, stk_b = sem("stk_a"), sem("stk_b")
    v_ps, v_sb = sem("v_ps"), sem("v_sb")
    q_ps, q_step = sem("q_ps"), sem("q_step")
    mx_ps, mx_done, m_col, m_ps, m_rows = (sem(s) for s in ("mx_ps", "mx_done", "m_col", "m_ps", "m_rows"))
    s_ps, p_sb, pv_done, o_sb, o_ps, o_step = (sem(s) for s in ("s_ps", "p_sb", "pv_done", "o_sb", "o_ps", "o_step"))
    QSTEPS, OSTEPS = 7, 5
    A_DMAS, B_DMAS = 13, 12

    def need(eng, s, value):
        if isinstance(value, int) and value <= 0:
            return
        eng.wait_ge(s, value)

    def free_bank(eng, b, pos, skipped):
        n, p = b, pos
        while True:
            p -= RING
            if p < 0:
                n, p = n - 1, max(q for q in range(len(UNITS)) if q % RING == pos % RING)
                if isinstance(n, int) and n < -1:
                    return
            kind, i = UNITS[p]
            if not skipped(kind, n):
                break
        m = n + 1
        if kind == "K":
            need(eng, k_hi, PER["K"] * m + i + 1)
            need(eng, k_32, PER["K"] * m + i + 1)
        elif kind == "V":
            need(eng, v_sb, PER["V"] * m + i + 1)
        elif kind == "Q":
            need(eng, q_step, QSTEPS * m + 1)
        elif kind == "MX":
            need(eng, mx_done, PER["MX"] * m + i + 1)
        elif kind == "MT":
            need(eng, m_rows, m + 1)
        elif kind == "OT":
            need(eng, o_step, OSTEPS * (n - 1) + 2)

    def skip_for(b):
        def skipped(kind, n):
            if isinstance(n, int):
                if kind == "OT":
                    return n < 1
                return n >= B - 1
            return False
        return skipped

    def items(b, attend, prepare, split):
        for kind, i in SCHEDULE:
            if kind in ("ST", "PV") and not attend:
                continue
            if kind in ("Q", "K", "V", "MX", "MT") and not prepare:
                continue
            if kind == "CH" and not split:
                continue
            if kind == "OT" and isinstance(b, int) and b < 1:
                continue
            yield kind, i, (UNITS.index((kind, i)) if (kind, i) in UNITS else None)

    def run(eng, body):
        body(-1, 1, False, True, False)
        body(0, 0, True, True, True)
        body(0, 1, True, True, True)
        with eng.Fori(1, B // 2 - 1) as g:
            body(g, 0, True, True, True)
            body(g, 1, True, True, True)
        body(B // 2 - 1, 0, True, True, False)
        body(B // 2 - 1, 1, True, False, False)

    block = ctx.enter_context(nc.Block())

    @block.sync
    def _(sp):
        for i, (name, landed) in enumerate((("wk_t", in_wk), ("wq_t", in_wq), ("wv_t", in_wv))):
            sp.dma_start(W_RAW[i], dram[name].rearrange("(k p) n -> p k n", p=P)).then_inc(landed, 16)
        sp.dma_start(X[:, :, :], dram["x"].rearrange("(t p) d -> p t d", p=P)).then_inc(in_x, 16)
        sp.dma_start(TOKI, dram["tok"].broadcast_to([B, LK])).then_inc(in_tok, 16)
        sp.dma_start(LENI[:, :], dram["lens"].broadcast_to([P, B])).then_inc(in_b, 16)
        sp.dma_start(LENPI[:, :], dram["lens"].rearrange("a b -> b a")).then_inc(in_b, 16)
        sp.dma_start(BQ[:, :], dram["bq"]).then_inc(in_b, 16)
        sp.dma_start(BK[:, :], dram["bk"]).then_inc(in_b, 16)
        sp.dma_start(BV[:, :], dram["bv"].rearrange("(a d) -> a d", a=1).broadcast_to([P, D])).then_inc(in_b, 16)

        def load(n):
            need(sp, ctx_lo, 2 * n)
            for k in range(KT):
                sp.dma_start(CTX[:, k, :], dram["ctx_t"][bass.ds(n, 1), k * P:(k + 1) * P, :].rearrange("a p t -> p (a t)"))\
                    .then_inc(in_ctx, 16)

        def stack(n, u, half):
            lo, hi = (0, HALF) if half == 0 else (HALF, LK)
            s = stk_a if half == 0 else stk_b
            if half == 0:
                sp.wait_ge(mask_out, 16)
                need(sp, s_ps, NT * (n - 1))
            need(sp, k_lo, PER["K"] * n + 4 * (half + 1))
            if half == 0:
                sp.dma_start(STK[u][ROW_MASK:ROW_MASK + 1, :, :],
                             dram["kmask"][bass.ds(n, 1), :].rearrange("a (o t) -> a o t", o=1).broadcast_to([1, PAIRS, LK]))\
                    .then_inc(s, 16)
            for c in range(4):
                rows = slice(32 * c, 32 * c + 32)
                for q, part in enumerate((K_HI, K_LO, K_HI)):
                    sp.dma_start(STK[u][32 * q:32 * q + 32, c::4, lo:hi], part[rows, :, lo:hi]).then_inc(s, 16)

        load(0)
        sp.dma_start(CST[:, :], dram["cst"]).then_inc(in_cst, 16)
        sp.wait_ge(mask_ready, 1)
        sp.dma_start(dram["kmask"], KMH).then_inc(mask_out, 16)
        load(1)
        sp.wait_ge(pool_init, 5)

        def body(g, u, attend, prepare, split):
            b = 2 * g + u
            if split:
                load(b + 2)
            if prepare:
                stack(b + 1, 1 - u, 0)
                stack(b + 1, 1 - u, 1)

        run(sp, body)

    @block.gpsimd
    def _(pool):
        pool.memset(MCOL[:, :], 0.0).then_inc(pool_init, 1)
        ones = float(np.ones(2, np.float16).view(np.float32)[0])
        for u in range(2):
            pool.wait_ge(pool_init, u + 1)
            pool.memset(STK_MEM[u][ROW_M:ROW_MASK, :].bitcast(F32), ones).then_inc(pool_init, 1)
        pool.wait_ge(pool_init, 3)
        pool.memset(V[0][:, :, :, DH:VW], 1.0).then_inc(pool_init, 1)
        pool.wait_ge(pool_init, 4)
        pool.wait_ge(mask_out, 16)
        pool.memset(V[1][:, :, :, DH:VW], 1.0).then_inc(pool_init, 1)

        def k_low(n, i):
            lo, hi = chunk(i // 2)
            pool.wait_ge(k_hi, PER["K"] * n + i + 1)
            pool.wait_ge(k_32, PER["K"] * n + i + 1)
            if i < 4:
                need(pool, stk_a, 16 * A_DMAS * n)
            else:
                need(pool, stk_b, 16 * B_DMAS * n)
            pool.tensor_tensor(K_LO[:, i % 2, lo:hi], K32[:, i % 2, 0:hi - lo], K_HI[:, i % 2, lo:hi],
                               ALU.subtract).then_inc(k_lo, 1)

        def ctx_low(n, u, half):
            lo, hi = (0, HALF) if half == 0 else (HALF, LK)
            pool.wait_ge(ctx_hi, 2 * n + half + 1)
            pool.tensor_tensor(CTX_LO[:, u, :, lo:hi], CTX[:, :, lo:hi], CTX_HI[:, u, :, lo:hi],
                               ALU.subtract).then_inc(ctx_lo, 1)

        pool.wait_ge(pool_init, 5)
        ctx_low(0, 0, 0)
        ctx_low(0, 0, 1)
        ctx_low(1, 1, 0)
        ctx_low(1, 1, 1)

        def body(g, u, attend, prepare, split):
            b = 2 * g + u
            for kind, i, _ in items(b, attend, prepare, split):
                if kind == "K":
                    k_low(b + 1, i)
                elif kind == "CH":
                    ctx_low(b + 2, u, i)

        run(pool, body)

    @block.tensor
    def _(pe):
        pe.wait_ge(in_cst, 16)
        for t in range(TILES):
            pe.wait_ge(xn_ready, t + 1)
            if t % 2 == 0 and t >= 4:
                pe.wait_ge(xt_lo, t // 2 - 1)
            for k in range(KT):
                last = pe.transpose(W_PS[t // 2 % 2][:, (2 * k + t % 2) * P:(2 * k + t % 2 + 1) * P],
                                    XN[:, t % 4, k * P:(k + 1) * P], CST[:, C_ID:C_ID + P])
            last.then_inc(xt_ps, 1)
        pe.wait_ge(xt_lo, TILES // 2)
        pe.wait_ge(wq_spread, 2)
        pe.wait_ge(w_step, 9)
        pe.wait_ge(init_done, 2)
        pe.wait_ge(pool_init, 5)

        def body(g, u, attend, prepare, split):
            b = 2 * g + u
            n, w = b + 1, 1 - u
            skipped = skip_for(b)
            for kind, i, pos in items(b, attend, prepare, split):
                if pos is not None:
                    if kind == "OT":
                        pe.wait_ge(in_cst, 16)
                    free_bank(pe, b, pos, skipped)
                    bank = W_PS[pos % RING]
                if kind == "ST":
                    par = (u + i) % 2
                    if i == 0:
                        pe.wait_ge(m_rows, b + 1)
                    need(pe, p_sb, NT * b + i - 1)
                    m = P if i < NT - 1 else LAST
                    for j in range(PAIRS):
                        last = pe.matmul(S_PS[par][0:m, j * 2 * SQ:(j + 1) * 2 * SQ],
                                         STK[u][0:KROWS, j, i * P:i * P + m], QS[0:KROWS, u, j, :, :],
                                         start=True, stop=True)
                    last.then_inc(s_ps, 1)
                elif kind == "PV":
                    par = (u + i) % 2
                    m = P if i < NT - 1 else LAST
                    if i == 0:
                        need(pe, o_sb, b)
                    pe.wait_ge(p_sb, NT * b + i + 1)
                    for h in range(H):
                        r = 32 * (h % 4)
                        last = pe.matmul(O_PS[r:r + VW, (h // 4) * SQ:(h // 4 + 1) * SQ],
                                         V[u][0:m, i, h, :], PR[0:m, par, h * SQ:(h + 1) * SQ],
                                         start=(i == 0 and h < 4), stop=(i == NT - 1), skip_group_check=True)
                    last.then_inc(pv_done, 1)
                elif kind == "K":
                    c, m = i // 2, i % 2
                    lo, hi = chunk(c)
                    pe.wait_ge(ctx_lo, 2 * n + (1 if c < 2 else 2))
                    parts = [(WK_HI, CTX_HI), (WK_HI, CTX_LO), (WK_LO, CTX_HI)]
                    for e, (a, c_) in enumerate([(x, k) for x in parts for k in range(KT)]):
                        last = pe.matmul(bank[:, 0:hi - lo], a[0][:, c_, m * P:(m + 1) * P], a[1][:, w, c_, lo:hi],
                                         start=(e == 0), stop=(e == 5))
                    last.then_inc(k_ps, 1)
                elif kind == "V":
                    for s in range(2 if i < 6 else 1):
                        t = 2 * i + s
                        lo, hi = t * P, min((t + 1) * P, LK)
                        parts = [(CTX_HI, WV_HI), (CTX_HI, WV_LO), (CTX_LO, WV_HI)]
                        for e, (a, k) in enumerate([(x, k) for k in range(KT) for x in parts]):
                            last = pe.matmul(bank[0:hi - lo, s * D:(s + 1) * D], a[0][:, w, k, lo:hi], a[1][:, k, :],
                                             start=(e == 0), stop=(e == 5), skip_group_check=True)
                    last.then_inc(v_ps, 1)
                elif kind == "Q":
                    for j in range(PAIRS):
                        parts = [(WQ_HI, XT_HI), (WQ_HI, XT_LO), (WQ_LO, XT_HI)]
                        for e, (a, k) in enumerate([(x, k) for x in parts for k in range(KT)]):
                            last = pe.matmul(bank[:, j * SQ:(j + 1) * SQ], a[0][:, k, j, :, :],
                                             a[1][:, k, bass.ds(n * SQ, SQ)], start=(e == 0), stop=(e == 5),
                                             skip_group_check=True)
                    last.then_inc(q_ps, 1)
                elif kind == "MX":
                    if i == 0:
                        pe.wait_ge(stk_a, 16 * A_DMAS * (n + 1))
                        pe.wait_ge(q_step, QSTEPS * (n + 1))
                    if i == 16:
                        pe.wait_ge(stk_b, 16 * B_DMAS * (n + 1))
                    if i < 24:
                        lo, hi = chunk(i // 8)
                        todo = [(i % 8, 0)]
                    else:
                        lo, hi = chunk(3)
                        todo = [((i - 24) * 4 + s, s) for s in range(4)]
                    for j, s in todo:
                        last = pe.matmul(bank[:, s * LAST:s * LAST + hi - lo], QS[0:KROWS, w, j, :, :],
                                         STK[w][0:KROWS, j, lo:hi], start=True, stop=True, skip_group_check=True)
                    last.then_inc(mx_ps, 1)
                elif kind == "MT":
                    pe.wait_ge(m_col, n + 1)
                    pe.transpose(bank[:, 0:P], MCOL[:, :], CST[:, C_ID:C_ID + P]).then_inc(m_ps, 1)
                elif kind == "OT":
                    pe.wait_ge(o_sb, b)
                    for g in range(4):
                        last = pe.transpose(bank[0:SQ, g * P:(g + 1) * P], OSB[:, g, :], CST[:, C_ID:C_ID + P])
                    last.then_inc(o_ps, 1)

        run(pe, body)
        pe.wait_ge(o_sb, B)
        pe.wait_ge(o_step, OSTEPS * (B - 2) + 2)
        for g in range(4):
            last = pe.transpose(W_PS[0][0:SQ, g * P:(g + 1) * P], OSB[:, g, :], CST[:, C_ID:C_ID + P])
        last.then_inc(o_ps, 1)

    @block.scalar
    def _(act):
        act.wait_ge(ln_stat, 2 * TILES + 1)
        nc.scalar.activation(SD[:, :], VE[:, :], ACT.Sqrt).then_inc(root_ready, 1)
        act.wait_ge(w_step, 6)
        for w in (WQ_HI, WQ_LO):
            rows = w[:, :, :, :, :].rearrange("p k j c n -> p (k j) c n")
            nc.scalar.activation(rows[:, :, 1:4, :], rows[:, :, 0:1, :].broadcast_to([P, KT * PAIRS, 3, 32]), ACT.Copy)\
                .then_inc(wq_spread, 1)
        for v in range(TILES // 2):
            act.wait_ge(xt_ps, 2 * v + 2)
            nc.scalar.activation(XT_HI[:, :, 2 * v * P:(2 * v + 2) * P], W_PS[v % 2][:, :].rearrange("p (k r) -> p k r", k=KT),
                                 ACT.Copy).then_inc(xt_hi, 1)
        act.wait_ge(in_b, 16 * 5)
        act.wait_ge(w_step, 9)
        act.wait_ge(pool_init, 5)

        def o_copy(b):
            act.wait_ge(pv_done, NT * (b + 1))
            need(act, o_ps, b)
            nc.scalar.activation(OSB[:, :, :], O_PS[:, 0:4 * SQ].rearrange("p (g q) -> p g q", g=4), ACT.Copy)\
                .then_inc(o_sb, 1)

        def body(g, u, attend, prepare, split):
            b = 2 * g + u
            n, w = b + 1, 1 - u
            for kind, i, pos in items(b, attend, prepare, split):
                bank = W_PS[pos % RING] if pos is not None else None
                if kind == "ST":
                    par = (u + i) % 2
                    m = P if i < NT - 1 else LAST
                    act.wait_ge(s_ps, NT * b + i + 1)
                    need(act, pv_done, NT * b + i - 1)
                    nc.scalar.activation(PR[0:m, par, :], S_PS[par][0:m, :], ACT.Exp).then_inc(p_sb, 1)
                elif kind == "K":
                    lo, hi = chunk(i // 2)
                    act.wait_ge(k_ps, PER["K"] * n + i + 1)
                    if i < 4:
                        need(act, stk_a, 16 * A_DMAS * n)
                    else:
                        need(act, stk_b, 16 * B_DMAS * n)
                    nc.scalar.activation(K_HI[:, i % 2, lo:hi], bank[:, 0:hi - lo], ACT.Identity,
                                         bias=BK[:, i % 2:i % 2 + 1], scale=1 / W_SCALE).then_inc(k_hi, 1)
                elif kind == "V":
                    act.wait_ge(v_ps, PER["V"] * n + i + 1)
                    need(act, pv_done, NT * (n - 1))
                    t0, t1, m = (2 * i, 2 * i + 2, P) if i < 6 else (12, 13, LAST)
                    nc.scalar.activation(V[w][0:m, t0:t1, :, 0:DH],
                                         bank[0:m, 0:(t1 - t0) * D].rearrange("p (t h d) -> p t h d", t=t1 - t0, h=H),
                                         ACT.Copy, scale=1 / W_SCALE).then_inc(v_sb, 1)
            if attend:
                o_copy(b)

        run(act, body)

    @block.vector
    def _(dve):
        dve.memset(O_PS[:, :], 0.0).then_inc(init_done, 1)

        def split_w(step, raw, hi, lo, landed):
            dve.wait_ge(landed, 16)
            dve.tensor_scalar(raw, raw, W_SCALE, None, ALU.mult).then_inc(w_step, 1)
            dve.wait_ge(w_step, step + 1)
            dve.tensor_copy(hi, raw).then_inc(w_step, 1)
            dve.wait_ge(w_step, step + 2)
            dve.tensor_tensor(lo, raw, hi, ALU.subtract).then_inc(w_step, 1)

        split_w(0, W_RAW[0], WK_HI[:, :, :], WK_LO[:, :, :], in_wk)
        wq = W_RAW[1].rearrange("p k (j n) -> p (k j) n", n=32)
        split_w(3, wq, *(w[:, :, :, 0, :].rearrange("p k j n -> p (k j) n") for w in (WQ_HI, WQ_LO)), in_wq)
        split_w(6, W_RAW[2], WV_HI[:, :, :], WV_LO[:, :, :], in_wv)
        dve.wait_ge(in_x, 16)
        for t in range(TILES):
            dve.bn_stats(STAT[:, t, :], X[:, t, :]).then_inc(ln_stat, 1)
        dve.wait_ge(ln_stat, TILES)
        for t in range(TILES):
            dve.bn_aggr(MV[:, t, :], STAT[:, t, :]).then_inc(ln_stat, 1)
        dve.wait_ge(ln_stat, 2 * TILES)
        dve.tensor_scalar(VE[:, :], MV[:, :, 1], LN_EPS, None, ALU.add).then_inc(ln_stat, 1)

        dve.wait_ge(in_b, 16 * 5)
        dve.tensor_copy(LEN[:, :], LENI[:, :]).then_inc(init_done, 1)
        dve.tensor_scalar(BQ[:, :], BQ[:, :], 0.25, None, ALU.mult).then_inc(ln_step, 1)
        dve.tensor_copy(LENP[:, :], LENPI[:, :]).then_inc(ln_step, 1)
        dve.wait_ge(ln_step, 2)
        dve.wait_ge(in_tok, 16)
        dve.tensor_scalar(KMH, TOKI, LENP[:, 0:1], -MASK, ALU.is_ge, ALU.mult).then_inc(mask_ready, 1)

        def ctx_high(n, u, half):
            lo, hi = (0, HALF) if half == 0 else (HALF, LK)
            dve.wait_ge(in_ctx, 16 * KT * (n + 1))
            need(dve, v_ps, PER["V"] * (n - 1))
            dve.tensor_copy(CTX_HI[:, u, :, lo:hi], CTX[:, :, lo:hi]).then_inc(ctx_hi, 1)

        ctx_high(0, 0, 0)
        ctx_high(0, 0, 1)
        inverse_deviation(dve, VE[:, :], SD[:, :], RSTD[:, :], VT[:, :], ln_stat, root_ready, 2 * TILES + 1)
        for t in range(TILES + 2):
            if t < TILES:
                if t >= 4:
                    dve.wait_ge(xt_ps, t - 3)
                dve.tensor_scalar(XN[:, t % 4, :], X[:, t, :], MV[:, t, 0:1], RSTD[:, t:t + 1],
                                  ALU.subtract, ALU.mult).then_inc(xn_ready, 1)
            if t % 2 and t >= 3:
                v = t // 2 - 1
                cols = slice(2 * v * P, (2 * v + 2) * P)
                dve.wait_ge(xt_hi, v + 1)
                dve.tensor_tensor(XT_LO[:, :, cols], W_PS[v % 2][:, :].rearrange("p (k r) -> p k r", k=KT),
                                  XT_HI[:, :, cols], ALU.subtract).then_inc(xt_lo, 1)
        ctx_high(1, 1, 0)
        ctx_high(1, 1, 1)

        def query_rows(n, w, bank, col):
            q = QSTEPS * n
            dve.wait_ge(q_ps, n + 1)
            if not isinstance(n, int) or n > 0:
                dve.wait_ge(q_step, q)
            dve.scalar_tensor_tensor(Q1[:, :, :], bank[:, :].rearrange("p (j q) -> p j q", j=PAIRS), 0.25 / W_SCALE,
                                     BQ[:, :].unsqueeze(2).broadcast_to([P, PAIRS, SQ]), ALU.mult, ALU.add).then_inc(q_step, 1)
            dve.wait_ge(q_step, q + 1)
            iq = CST[:, C_IQ:C_IQ + SQ].unsqueeze(1).broadcast_to([P, PAIRS, SQ])
            dve.scalar_tensor_tensor(Q2[:, :, :], iq, LEN[:, col], Q1[:, :, :], ALU.is_lt, ALU.mult).then_inc(q_step, 1)
            dve.wait_ge(q_step, q + 2)
            dve.tensor_copy(QU[0:96], Q2[0:96]).then_inc(q_step, 1)
            dve.wait_ge(q_step, q + 3)
            dve.tensor_tensor(QU[64:96], Q2[64:96], QU[64:96], ALU.subtract).then_inc(q_step, 1)
            dve.wait_ge(q_step, q + 4)
            need(dve, s_ps, NT * (n - 1))
            for a in range(2):
                dve.tensor_scalar(QS[0:96, w, :, a, :], QU[0:96], CST[0:96, C_HM + a:C_HM + a + 1], None,
                                  ALU.mult).then_inc(q_step, 1)
            ie = CST[ROW_M:P, C_IQ:C_IQ + SQ].unsqueeze(1).broadcast_to([32, H, SQ])
            dve.tensor_scalar(QS[ROW_M:P, w, :, :, :].rearrange("p j a q -> p (j a) q"), ie, LEN[ROW_M:P, col],
                              CST[ROW_M:P, C_EXT:C_EXT + 1], ALU.is_lt, ALU.mult).then_inc(q_step, 1)

        def part_max(n, i, bank):
            dve.wait_ge(mx_ps, PER["MX"] * n + i + 1)
            if i == 0:
                need(dve, m_col, n)
            if i < 24:
                dve.tensor_reduce(MXP[:, i % 8, i // 8:i // 8 + 1], bank[:, :], AX.X, ALU.max).then_inc(mx_done, 1)
            else:
                g = 4 * (i - 24)
                dve.tensor_reduce(MXP[:, g:g + 4, 3], bank[:, 0:4 * LAST].rearrange("p (j t) -> p j t", j=4),
                                  AX.X, ALU.max).then_inc(mx_done, 1)
            if i == PER["MX"] - 1:
                dve.wait_ge(mx_done, PER["MX"] * (n + 1))
                need(dve, m_ps, n)
                dve.tensor_reduce(MCOL[:, ROW_M:ROW_M + PAIRS], MXP[:, :, :], AX.X, ALU.max).then_inc(m_col, 1)

        def max_rows(n, w, bank):
            dve.wait_ge(m_ps, n + 1)
            rows = slice(ROW_M, ROW_M + PAIRS)
            dve.tensor_tensor(QS[rows, w].rearrange("p j a q -> p j (a q)"),
                              bank[rows, 0:P].unsqueeze(1).broadcast_to([PAIRS, PAIRS, P]),
                              CST[rows, C_DM:C_DM + PAIRS].unsqueeze(2).broadcast_to([PAIRS, PAIRS, P]),
                              ALU.mult).then_inc(m_rows, 1)

        def out_rows(b, u, tile, bank):
            o = OSTEPS * b
            rows = slice(64 * u, 64 * u + 64)
            dve.wait_ge(o_ps, b + 1)
            if not isinstance(b, int) or b > 0:
                dve.wait_ge(o_step, o)
            heads = bank[0:SQ, :].rearrange("p (h d) -> p h d", h=H)
            dve.reciprocal(RDEN[rows, :], heads[:, :, DH]).then_inc(o_step, 1)
            dve.wait_ge(o_step, o + 1)
            dve.tensor_tensor(OTMP[rows], heads[:, :, 0:DH], RDEN[rows, :].unsqueeze(2).broadcast_to([SQ, H, DH]),
                              ALU.mult).then_inc(o_step, 1)
            dve.wait_ge(o_step, o + 2)
            o2 = OTMP[rows].rearrange("p h d -> p (h d)")
            dve.tensor_tensor(o2, o2, BV[rows, :], ALU.add).then_inc(o_step, 1)
            dve.wait_ge(o_step, o + 3)
            xr = X[rows, bass.ds(tile, 1), :].rearrange("p a d -> p (a d)")
            dve.tensor_tensor(xr, xr, o2, ALU.add).then_inc(o_step, 1)
            dve.wait_ge(o_step, o + 4)
            dve.bn_stats(STAT[rows, bass.ds(tile, 1), :].rearrange("p a s -> p (a s)"), xr).then_inc(o_step, 1)

        dve.wait_ge(in_cst, 16)
        dve.wait_ge(init_done, 2)

        def body(g, u, attend, prepare, split):
            b = 2 * g + u
            n, w = b + 1, 1 - u
            for kind, i, pos in items(b, attend, prepare, split):
                bank = W_PS[pos % RING] if pos is not None else None
                if kind == "K":
                    lo, hi = chunk(i // 2)
                    dve.wait_ge(k_hi, PER["K"] * n + i + 1)
                    need(dve, k_lo, PER["K"] * n + i - 1)
                    dve.tensor_scalar(K32[:, i % 2, 0:hi - lo], bank[:, 0:hi - lo], 1 / W_SCALE, BK[:, i % 2:i % 2 + 1],
                                      ALU.mult, ALU.add).then_inc(k_32, 1)
                elif kind == "Q":
                    query_rows(n, w, bank, bass.ds(n, 1))
                elif kind == "MX":
                    part_max(n, i, bank)
                elif kind == "MT":
                    max_rows(n, w, bank)
                elif kind == "OT":
                    out_rows(b - 1, 1 - u, g - 1 + u, bank)
                elif kind == "CH":
                    ctx_high(b + 2, u, i)

        run(dve, body)
        out_rows(B - 1, 1, TILES - 1, W_PS[0])
        dve.wait_ge(o_step, OSTEPS * B)


def deviations(dve, stat, mv, ve, sd, r, t, step, root_ready, base=0):
    for i in range(TILES):
        dve.bn_aggr(mv[:, i, :], stat[:, i, :]).then_inc(step, 1)
    dve.wait_ge(step, base + TILES)
    dve.tensor_scalar(ve, mv[:, :, 1], LN_EPS, None, ALU.add).then_inc(step, 1)
    inverse_deviation(dve, ve, sd, r, t, step, root_ready, base + TILES + 1)
    dve.scalar_tensor_tensor(t, mv[:, :, 0], -1.0, r, ALU.mult, ALU.mult).then_inc(step, 1)


LN_ROOT = TILES + 1
LN_STEPS = TILES + 7


def self_attention(nc, sb, ctx, dram):
    def alloc(name, shape, dt):
        return ctx.enter_context(nc.sbuf_tensor(name, shape, dt))

    def psum(name, shape):
        return ctx.enter_context(nc.psum_tensor(name, shape, F32))

    def sem(name):
        return ctx.enter_context(nc.semaphore(name))

    X, CST, STAT = sb["X"], sb["CST"], sb["STAT"]
    XN = alloc("XN2", [P, TILES, D], F32)
    XHI = alloc("XHI", [P, KT, ROWS], F16)
    XLO = alloc("XLO", [P, KT, ROWS], F16)
    MV = alloc("MV2", [P, TILES, 2], F32)
    VE, SD, RS, VT = (alloc(s, [P, TILES], F32) for s in ("VE2", "SD2", "RS2", "VT2"))
    WRAW = alloc("WRAW2", [P, KT, 3 * D], F32)
    WHI = alloc("WHI2", [P, KT, 3 * D], F16)
    WLO = alloc("WLO2", [P, KT, 3 * D], F16)
    BQK = alloc("BQK", [P, 4], F32)
    BV = alloc("BV2", [P, D], F32)
    BP, LG, LB = (alloc(s, [P, D], F32) for s in ("BP", "LG", "LB"))
    WP = alloc("WP", [P, 4, D], F32)
    BIAS = alloc("BIAS", [P, PAIRS, SQ], F32)
    QK_HI = alloc("QK_HI", [P, 4, ROWS], F16)
    QK_LO = alloc("QK_LO", [P, 4, ROWS], F16)
    QK32 = alloc("QK32", [P, 2, CH], F32)
    V = alloc("V2", [P, TILES, D], F32)
    VS = alloc("VS", [P, 2, 2, D], F32)
    SK = alloc("SK", [96, PAIRS, ROWS], F16)
    SQS = alloc("SQS", [96, PAIRS, ROWS], F16)
    QZ = alloc("QZ", [96, 2, PAIRS, 2, 2, SQ], F16)
    T = alloc("T", [P, 2, PAIRS, 2, SQ], F32)
    MX = alloc("MX2", [P, 2, PAIRS, 2], F32)
    SM = alloc("SM2", [P, 2, PAIRS, 2], F32)
    PT = XHI[:, :, :].rearrange("p k r -> p (k r)").bitcast(F32).rearrange("p (u j r) -> p u j r", u=2, j=PAIRS)
    OT = XLO[:, 0, :].bitcast(F32).rearrange("p (u g r) -> p u g r", u=2, g=4)

    S_PS = [psum(f"S2_PS{i}", [P, 1024]) for i in range(2)]
    T_PS = psum("T2_PS", [P, 1024])
    O_PS = psum("O2_PS", [P, 512])
    Y_PS = psum("Y2_PS", [P, 512])
    RINGS = [S_PS[0][:, 0:512], S_PS[0][:, 512:1024], S_PS[1][:, 0:512], S_PS[1][:, 512:1024]]

    names = ("in_w2 in_small in_wp ln2 root2 tr_ps tr_hi tr_lo w2 qk_ps qk_hi qk_32 qk_lo v2_ps v2_sb stacked "
             "vs bias_ok bp_added zeroed s2_ps qz t_a t_max t_sub t_exp t_sum t_norm p2_ps pt_sb pv2 ot_sb y_ps y_sb "
             "xn2 y_stat ln2b root2b y_normal y_scaled x2_done b_done").split()
    sm = {s: sem(s) for s in names}
    N_SMALL = 6

    block = ctx.enter_context(nc.Block())

    @block.sync
    def _(sp):
        sp.dma_start(WRAW[:, :, :], dram["w_t"].rearrange("(k p) n -> p k n", p=P)).then_inc(sm["in_w2"], 16)
        sp.dma_start(BQK[:, :], dram["bqk"]).then_inc(sm["in_small"], 16)
        for tile, name in ((BV, "bv2"), (BP, "bp"), (LG, "ln_g"), (LB, "ln_b")):
            sp.dma_start(tile[:, :], dram[name].rearrange("(a d) -> a d", a=1).broadcast_to([P, D])).then_inc(sm["in_small"], 16)
        sp.dma_start(BIAS[:, :, :], dram["bias"]).then_inc(sm["in_small"], 16)
        sp.dma_start(WP[:, :, :], dram["wp"]).then_inc(sm["in_wp"], 16)
        for dst, m0, parts in ((SK, 2, (QK_HI, QK_LO, QK_HI)), (SQS, 0, (QK_HI, QK_HI, QK_LO))):
            units = 8 if m0 == 2 else 16
            sp.wait_ge(sm["qk_hi"], units)
            sp.wait_ge(sm["qk_lo"], units)
            for c in range(4):
                for q, part in enumerate(parts):
                    sp.dma_start(dst[32 * q:32 * q + 32, c::4, :], part[32 * c:32 * c + 32, m0:m0 + 2, :])\
                        .then_inc(sm["stacked"], 16)
        sp.wait_ge(sm["stacked"], 16 * 24)

    def qk_unit(i):
        return (2 if i < 8 else 0) + i % 2, i % 8 // 2 * CH

    def steps(eng, body):
        for s in range(4):
            body(s, s % 2)
        with eng.Fori(2, TILES // 2 - 1) as g:
            body(2 * g, 0)
            body(2 * g + 1, 1)
        for s in range(TILES - 2, TILES + 3):
            body(s, s % 2)

    def live(s, lag):
        return not isinstance(s, int) or 0 <= s - lag < TILES

    def need(eng, s, value):
        if isinstance(value, int) and value <= 0:
            return
        eng.wait_ge(s, value)

    @block.tensor
    def _(pe):
        for t in range(TILES):
            pe.wait_ge(sm["xn2"], t + 1)
            if t % 2 == 0 and t >= 4:
                pe.wait_ge(sm["tr_lo"], t // 2 - 1)
            for k in range(KT):
                last = pe.transpose(RINGS[t // 2 % 2][:, (2 * k + t % 2) * P:(2 * k + t % 2 + 1) * P],
                                    XN[:, t, k * P:(k + 1) * P], CST[:, C_ID:C_ID + P])
            last.then_inc(sm["tr_ps"], 1)
        pe.wait_ge(sm["w2"], 3)
        for i in range(16):
            m, lo = qk_unit(i)
            pe.wait_ge(sm["tr_lo"], 2 * (lo // CH) + 2)
            if i >= 2:
                pe.wait_ge(sm["qk_32"], i - 1)
            parts = [(WHI, XHI), (WHI, XLO), (WLO, XHI)]
            for e, (a, k) in enumerate([(x, k) for x in parts for k in range(KT)]):
                last = pe.matmul(RINGS[2 + i % 2], a[0][:, k, m * P:(m + 1) * P], a[1][:, k, lo:lo + CH],
                                 start=(e == 0), stop=(e == 5))
            last.then_inc(sm["qk_ps"], 1)
        for v in range(TILES // 2):
            if v < 2:
                pe.wait_ge(sm["tr_lo"], TILES // 2)
            else:
                pe.wait_ge(sm["v2_sb"], v - 1)
            for s in range(2):
                lo = (2 * v + s) * P
                parts = [(XHI, WHI), (XHI, WLO), (XLO, WHI)]
                for e, (a, k) in enumerate([(x, k) for k in range(KT) for x in parts]):
                    last = pe.matmul(RINGS[v % 2][:, s * D:(s + 1) * D], a[0][:, k, lo:lo + P], a[1][:, k, 2 * D:3 * D],
                                     start=(e == 0), stop=(e == 5), skip_group_check=True)
            last.then_inc(sm["v2_ps"], 1)
        pe.wait_ge(sm["stacked"], 16 * 24)
        pe.wait_ge(sm["v2_sb"], TILES // 2)
        pe.wait_ge(sm["qk_32"], 16)
        pe.wait_ge(sm["zeroed"], 2)
        pe.wait_ge(sm["in_wp"], 16)

        def body(s, u):
            if live(s, 0):
                pe.wait_ge(sm["qz"], 2 * s + 2)
                need(pe, sm["t_a"], 2 * s - 2)
                for j in range(PAIRS):
                    for w in range(2):
                        last = pe.matmul(S_PS[u][:, (2 * j + w) * SQ:(2 * j + w + 1) * SQ],
                                         QZ[:, u, j, w, :, :],
                                         SK[:, j, bass.ds(s * P + w * SQ, SQ)], start=True, stop=True, skip_group_check=True)
                last.then_inc(sm["s2_ps"], 1)
            if live(s, 2):
                t = s - 2
                pe.wait_ge(sm["pt_sb"], t + 1)
                pe.wait_ge(sm["vs"], 2 * t + 2)
                need(pe, sm["ot_sb"], t)
                for w in range(2):
                    for h in range(H):
                        r = 32 * (h % 4)
                        last = pe.matmul(O_PS[r:r + DH, (h // 4) * P + w * SQ:(h // 4) * P + (w + 1) * SQ],
                                         VS[:, u, w, h * DH:(h + 1) * DH],
                                         PT[:, u, h // 2, (h % 2) * SQ:(h % 2 + 1) * SQ],
                                         start=True, stop=True, skip_group_check=True)
                last.then_inc(sm["pv2"], 1)
            if live(s, 3):
                t = s - 3
                pe.wait_ge(sm["ot_sb"], t + 1)
                need(pe, sm["y_sb"], t)
                for g in range(4):
                    last = pe.matmul(Y_PS[:, 0:D], OT[:, 1 - u, g, :], WP[:, g, :], start=(g == 0), stop=(g == 3))
                last.then_inc(sm["y_ps"], 1)
            if live(s, 1):
                t = s - 1
                pe.wait_ge(sm["t_norm"], t + 1)
                need(pe, sm["pt_sb"], t)
                for j in range(PAIRS):
                    last = pe.transpose(T_PS[:, j * P:(j + 1) * P], T[:, 1 - u, j, :, :].rearrange("p w k -> p (w k)"),
                                        CST[:, C_ID:C_ID + P])
                last.then_inc(sm["p2_ps"], 1)

        steps(pe, body)

    @block.scalar
    def _(act):
        act.wait_ge(sm["ln2"], LN_ROOT)
        nc.scalar.activation(SD[:, :], VE[:, :], ACT.Sqrt).then_inc(sm["root2"], 1)
        for v in range(TILES // 2):
            act.wait_ge(sm["tr_ps"], 2 * v + 2)
            nc.scalar.activation(XHI[:, :, 2 * v * P:(2 * v + 2) * P], RINGS[v % 2].rearrange("p (k r) -> p k r", k=KT),
                                 ACT.Copy).then_inc(sm["tr_hi"], 1)
        act.wait_ge(sm["in_small"], 16 * N_SMALL)
        for i in range(16):
            m, lo = qk_unit(i)
            act.wait_ge(sm["qk_ps"], i + 1)
            nc.scalar.activation(QK_HI[:, m, lo:lo + CH], RINGS[2 + i % 2], ACT.Identity,
                                 bias=BQK[:, m:m + 1], scale=1 / W_SCALE).then_inc(sm["qk_hi"], 1)

        act.wait_ge(sm["v2_sb"], TILES // 2)
        act.wait_ge(sm["zeroed"], 2)
        def body(s, u):
            if live(s, 2):
                t = s - 2
                act.wait_ge(sm["p2_ps"], t + 1)
                need(act, sm["pv2"], t - 1)
                nc.scalar.activation(PT[:, u, :, :], T_PS[:, :].rearrange("p (j r) -> p j r", j=PAIRS), ACT.Copy)\
                    .then_inc(sm["pt_sb"], 1)
            if live(s, 2):
                t = s - 2
                act.wait_ge(sm["pv2"], t + 1)
                need(act, sm["y_ps"], t - 1)
                nc.scalar.activation(OT[:, u, :, :], O_PS[:, :].rearrange("p (g r) -> p g r", g=4), ACT.Copy)\
                    .then_inc(sm["ot_sb"], 1)
            if live(s, 1):
                t = s - 1
                need(act, sm["pv2"], t - 1)
                for w in range(2):
                    rows = slice(64 * w, 64 * w + 64)
                    nc.scalar.activation(VS[rows, 1 - u, w, :], V[rows, bass.ds(t, 1), :].rearrange("p a d -> p (a d)"), ACT.Copy)\
                        .then_inc(sm["vs"], 1)
            if live(s, 0):
                act.wait_ge(sm["t_sub"], s + 1)
                nc.scalar.activation(T[:, u], T[:, u], ACT.Exp).then_inc(sm["t_exp"], 1)

        steps(act, body)
        act.wait_ge(sm["ln2b"], LN_ROOT)
        nc.scalar.activation(SD[:, :], VE[:, :], ACT.Sqrt).then_inc(sm["root2b"], 1)
        act.wait_ge(sm["ln2b"], LN_STEPS)
        for i in range(TILES):
            nc.scalar.activation(XN[:, i, :], XN[:, i, :], ACT.Identity, bias=VT[:, i:i + 1], scale=RS[:, i:i + 1])\
                .then_inc(sm["y_normal"], 1)

    @block.gpsimd
    def _(pool):
        pool.wait_ge(sm["in_small"], 16 * N_SMALL)
        for a in range(2):
            b = BIAS[64 * a:64 * a + 64, :, :]
            pool.affine_select(b, b, pattern=[[0, PAIRS], [-1, SQ]], compare_op=ALU.is_ge, fill=-1e30, base=0,
                               channel_multiplier=1).then_inc(sm["bias_ok"], 1)
            pool.wait_ge(sm["bias_ok"], a + 1)
        for i in range(16):
            m, lo = qk_unit(i)
            pool.wait_ge(sm["qk_32"], i + 1)
            pool.tensor_tensor(QK_LO[:, m, lo:lo + CH], QK32[:, i % 2, :], QK_HI[:, m, lo:lo + CH], ALU.subtract)\
                .then_inc(sm["qk_lo"], 1)
        pool.wait_ge(sm["tr_ps"], TILES)
        pool.tensor_tensor(XN[:, :, :], XN[:, :, :], BP[:, :].unsqueeze(1).broadcast_to([P, TILES, D]), ALU.add)\
            .then_inc(sm["bp_added"], 1)

        def body(s, u):
            if live(s, 1):
                t = s - 1
                pool.wait_ge(sm["t_sum"], 2 * t + 2)
                pool.tensor_tensor(T[:, 1 - u], T[:, 1 - u], SM[:, 1 - u].unsqueeze(3).broadcast_to([P, PAIRS, 2, SQ]),
                                   ALU.mult).then_inc(sm["t_norm"], 1)
            if live(s, 0):
                pool.wait_ge(sm["t_max"], s + 1)
                pool.tensor_tensor(T[:, u], T[:, u], MX[:, u].unsqueeze(3).broadcast_to([P, PAIRS, 2, SQ]),
                                   ALU.subtract).then_inc(sm["t_sub"], 1)

        steps(pool, body)
        pool.tensor_tensor(X[:, :, :], X[:, :, :], LB[:, :].unsqueeze(1).broadcast_to([P, TILES, D]), ALU.add)\
            .then_inc(sm["b_done"], 1)
        for i in range(TILES):
            pool.wait_ge(sm["y_normal"], i + 1)
            pool.tensor_tensor(XN[:, i, :], XN[:, i, :], LG[:, :], ALU.mult).then_inc(sm["y_scaled"], 1)

    @block.vector
    def _(dve):
        deviations(dve, STAT, MV, VE[:, :], SD[:, :], RS[:, :], VT[:, :], sm["ln2"], sm["root2"])
        for i in range(TILES):
            dve.tensor_scalar(XN[:, i, :], X[:, i, :], MV[:, i, 0:1], RS[:, i:i + 1], ALU.subtract, ALU.mult)\
                .then_inc(sm["xn2"], 1)
        dve.wait_ge(sm["in_w2"], 16)
        dve.tensor_scalar(WRAW[:, :, :], WRAW[:, :, :], W_SCALE, None, ALU.mult).then_inc(sm["w2"], 1)
        dve.wait_ge(sm["w2"], 1)
        dve.tensor_copy(WHI[:, :, :], WRAW[:, :, :]).then_inc(sm["w2"], 1)
        dve.wait_ge(sm["w2"], 2)
        dve.tensor_tensor(WLO[:, :, :], WRAW[:, :, :], WHI[:, :, :], ALU.subtract).then_inc(sm["w2"], 1)
        for v in range(TILES // 2):
            cols = slice(2 * v * P, (2 * v + 2) * P)
            dve.wait_ge(sm["tr_hi"], v + 1)
            dve.tensor_tensor(XLO[:, :, cols], RINGS[v % 2].rearrange("p (k r) -> p k r", k=KT), XHI[:, :, cols],
                              ALU.subtract).then_inc(sm["tr_lo"], 1)
        dve.memset(O_PS[:, :], 0.0).then_inc(sm["zeroed"], 1)
        dve.memset(VS[:, :, :, :], 0.0).then_inc(sm["zeroed"], 1)
        dve.wait_ge(sm["zeroed"], 2)
        dve.wait_ge(sm["in_small"], 16 * N_SMALL)
        for i in range(16):
            m = qk_unit(i)[0]
            dve.wait_ge(sm["qk_hi"], i + 1)
            if i >= 2:
                dve.wait_ge(sm["qk_lo"], i - 1)
            dve.tensor_scalar(QK32[:, i % 2, :], RINGS[2 + i % 2], 1 / W_SCALE, BQK[:, m:m + 1], ALU.mult, ALU.add)\
                .then_inc(sm["qk_32"], 1)
        for v in range(TILES // 2):
            dve.wait_ge(sm["v2_ps"], v + 1)
            dve.scalar_tensor_tensor(V[:, 2 * v:2 * v + 2, :], RINGS[v % 2].rearrange("p (t d) -> p t d", t=2), 1 / W_SCALE,
                                     BV[:, :].unsqueeze(1).broadcast_to([P, 2, D]), ALU.mult, ALU.add).then_inc(sm["v2_sb"], 1)
        dve.wait_ge(sm["v2_sb"], TILES // 2)
        dve.wait_ge(sm["stacked"], 16 * 24)
        dve.wait_ge(sm["bias_ok"], 2)
        dve.wait_ge(sm["bp_added"], 1)

        def queries(s, u):
            need(dve, sm["s2_ps"], s - 1)
            for a in range(2):
                dve.tensor_scalar(QZ[:, u, :, :, a, :],
                                  SQS[:, :, bass.ds(s * P, P)].rearrange("p j (w q) -> p j w q", w=2),
                                  CST[0:96, C_HM + a:C_HM + a + 1], None, ALU.mult).then_inc(sm["qz"], 1)

        queries(0, 0)

        def body(s, u):
            if live(s, 1):
                t = s - 1
                dve.wait_ge(sm["t_exp"], t + 1)
                need(dve, sm["t_norm"], t - 1)
                dve.tensor_reduce(SM[:, 1 - u], T[:, 1 - u], AX.X, ALU.add).then_inc(sm["t_sum"], 1)
                dve.wait_ge(sm["t_sum"], 2 * t + 1)
                dve.reciprocal(SM[:, 1 - u], SM[:, 1 - u]).then_inc(sm["t_sum"], 1)
            if live(s, 0):
                dve.wait_ge(sm["s2_ps"], s + 1)
                need(dve, sm["p2_ps"], s - 1)
                for w in range(2):
                    dve.scalar_tensor_tensor(T[:, u, :, w, :],
                                             S_PS[u][:, :].rearrange("p (j w k) -> p j w k", j=PAIRS, w=2)[:, :, w, :],
                                             1 / 16, BIAS[:, :, :], ALU.mult, ALU.add).then_inc(sm["t_a"], 1)
                dve.wait_ge(sm["t_a"], 2 * s + 2)
                need(dve, sm["t_sub"], s - 1)
                dve.tensor_reduce(MX[:, u], T[:, u], AX.X, ALU.max).then_inc(sm["t_max"], 1)
            if live(s, -1):
                queries(s + 1, 1 - u)
            if live(s, 3):
                t = s - 3
                dve.wait_ge(sm["y_ps"], t + 1)
                y = XN[:, bass.ds(t, 1), :].rearrange("p a d -> p (a d)")
                dve.tensor_tensor(y, Y_PS[:, 0:D], y, ALU.add).then_inc(sm["y_sb"], 1)
                dve.wait_ge(sm["y_sb"], t + 1)
                dve.bn_stats(STAT[:, bass.ds(t, 1), :].rearrange("p a s -> p (a s)"), y).then_inc(sm["y_stat"], 1)

        steps(dve, body)
        dve.wait_ge(sm["y_stat"], TILES)
        deviations(dve, STAT, MV, VE[:, :], SD[:, :], RS[:, :], VT[:, :], sm["ln2b"], sm["root2b"])
        dve.wait_ge(sm["b_done"], 1)
        for i in range(TILES + 1):
            if i < TILES:
                dve.wait_ge(sm["y_scaled"], i + 1)
                dve.tensor_tensor(X[:, i, :], XN[:, i, :], X[:, i, :], ALU.add).then_inc(sm["x2_done"], 1)
            if i:
                dve.wait_ge(sm["x2_done"], i)
                dve.bn_stats(STAT[:, i - 1, :], X[:, i - 1, :]).then_inc(sm["y_stat"], 1)
        dve.wait_ge(sm["y_stat"], 2 * TILES)




INNER = 768
FT = INNER // P
WBLOCK = 32
A_MAX = 32767.0
W_MAX = 7.0
TINY = 1e-12
U16 = 65536.0


def feed_forward(nc, sb, ctx, dram):
    def alloc(name, shape, dt):
        return ctx.enter_context(nc.sbuf_tensor(name, shape, dt))

    def psum(name, shape):
        return ctx.enter_context(nc.psum_tensor(name, shape, F32))

    X, CST = sb["X"], sb["CST"]
    NBLK = INNER * D // P // WBLOCK
    XN = alloc("XN3", [P, TILES, D], F32)
    XT_HI, XT_LO = alloc("XT3_HI", [P, KT, ROWS], F16), alloc("XT3_LO", [P, KT, ROWS], F16)
    MV = alloc("MV3", [P, TILES, 2], F32)
    VE, SD, RS, VT = (alloc(s, [P, TILES], F32) for s in ("VE3", "SD3", "RS3", "VT3"))
    WN = alloc("WN", [P, 3, INNER * D // P], F32)
    WS = alloc("WS", [P, 3, NBLK], F32)
    WI = alloc("WI", [P, 3, NBLK], F32)
    WUT, WGT = ([alloc(f"{s}_{h}", [P, KT, INNER], F16) for h in ("HI", "LO")] for s in ("WUT", "WGT"))
    WDT = [alloc(f"WDT_{h}", [P, FT, D], F16) for h in ("HI", "LO")]
    U = alloc("U", [P, FT, ROWS], F32)
    G = alloc("G", [P, FT, ROWS], F32)
    SG = alloc("SG", [P, 3, ROWS], F32)
    GS = U[:, :, :].rearrange("p f r -> p (f r)").bitcast(F16).rearrange("p (a f r) -> p a f r", a=2, f=FT)
    AM = alloc("AM", [P, 5, 24], F32)
    AC = alloc("AC", [P, 5], F32)
    A1 = alloc("A1", [1, 5], F32)
    ONE = alloc("ONE", [1, P], F32)
    WORTH = alloc("WORTH", [P, 5], F32)
    SC = alloc("SC", [P, 5], F32)
    INV = alloc("INV", [P, 5], F32)
    RND = alloc("RND", [P, 3], F32)
    SCD = RND[:, 2:3]
    W_PS = [psum(f"W3_PS{i}", [P, 512]) for i in range(6)]
    M_PS = psum("M3_PS", [P, 512])
    M2_PS = psum("M4_PS", [P, 512])
    WT_PS = [M_PS, M2_PS]
    TURN = {12: 1, 18: 2}
    U_SCALED = 3
    U_STEPS = {5 + 2 * f: f for f in range(FT)}
    U_WHOLE = {7 + 2 * f: f for f in range(FT)}
    ON_POOL = (0, 1, 3, 4)
    OUT_ON_POOL = (2, 4)
    STEPS_ON_DVE = (0, 2, 5)
    OUT_COLS = [(0, 256), (256, 512), (512, 1024), (1024, 1536), (1536, 2048)]
    OUT_TURN = [1, 1, 2, 2] + [t // 4 + 2 for t in range(4, TILES)]

    names = ("in_wn ln3 xn3 xm root3 w_max w_step wt_ps wt_hi wt_lo const acol am_ps am1 ab_ps sc scale xr xt_ps xt_hi xt_lo "
             "up_ps up_sb ga_ps ga_sb um gm ur ui gr grv gi sg1 sg2 sg3 g2 g2v g2m g2r om or_ oh oi g2i o_v o_p dn_ps dn_sb out3").split()
    sm = {s: ctx.enter_context(nc.semaphore(s)) for s in names}
    in_wn = [ctx.enter_context(nc.semaphore(f"in_wn{i}")) for i in range(3)]
    CHUNKS = FT * ROWS // CH
    WSTEPS = 4
    SSTEPS = 5

    def gate_done(f):
        if f in ON_POOL:
            return sm["g2"], ON_POOL.index(f) + 1
        return sm["g2v"], sum(x not in ON_POOL for x in range(f + 1))

    def unit(t, i):
        return t[:, i // 4, i % 4 * CH:(i % 4 + 1) * CH]

    block = ctx.enter_context(nc.Block())
    weights = [(WUT, FT, KT), (WGT, FT, KT), (WDT, KT, FT)]

    def groups(w):
        dst, outs, ins = weights[w]
        return [(k, range(o, min(o + 3, outs))) for k in range(ins) for o in range(0, outs, 3)]

    WT_DONE = [len(groups(0)), len(groups(0)) + len(groups(1)), sum(len(groups(w)) for w in range(3))]

    @block.sync
    def _(sp):
        for w, name in enumerate(("w_up", "w_gate", "w_down")):
            f = (FT, FT, KT)[w]
            sp.dma_start(WN[:, w, :].rearrange("p (f d) -> p f d", f=f), dram[name].rearrange("(f p) d -> p f d", p=P))\
                .then_inc(in_wn[w], 16)
        for i in range(TILES // 4):
            sp.wait_ge(sm["dn_sb"], 4 * i + 4)
            sp.dma_start(dram["out"][4 * i * P:(4 * i + 4) * P, :].rearrange("(t p) d -> p t d", p=P), X[:, 4 * i:4 * i + 4, :])\
                .then_inc(sm["out3"], 16)
        sp.wait_ge(sm["out3"], 16 * (TILES // 4))

    @block.gpsimd
    def _(pool):
        for w in range(3):
            blk = WN[:, w, :].rearrange("p (b e) -> p b e", e=WBLOCK)
            n = WSTEPS * w
            pool.wait_ge(sm["w_max"], 3 * w + 3)

            def wide(t):
                return t[:, w, :].unsqueeze(2).broadcast_to([P, NBLK, WBLOCK])

            pool.tensor_tensor(blk, blk, wide(WI), ALU.mult).then_inc(sm["w_step"], 1)
            pool.wait_ge(sm["w_step"], n + 1)
            pool.tensor_scalar(blk, blk, ROUND, ROUND, ALU.add, ALU.subtract).then_inc(sm["w_step"], 1)
            pool.wait_ge(sm["w_step"], n + 2)
            pool.tensor_scalar(blk, blk, -W_MAX - 1, W_MAX, ALU.max, ALU.min).then_inc(sm["w_step"], 1)
            pool.wait_ge(sm["w_step"], n + 3)
            pool.tensor_tensor(blk, blk, wide(WS), ALU.mult).then_inc(sm["w_step"], 1)
        for f in ON_POOL:
            pool.wait_ge(sm["sg3"], f + 1)
            pool.tensor_tensor(G[:, f, :], G[:, f, :], SG[:, f % 3, :], ALU.mult).then_inc(sm["g2"], 1)
        for n, f in enumerate(OUT_ON_POOL):
            pool.wait_ge(sm["g2i"], n + 1)
            pool.tensor_tensor(G[:, f, :], G[:, f, :], U[:, f, :], ALU.mult).then_inc(sm["o_p"], 1)

    @block.tensor
    def _(pe):
        count = [0]

        def turn_weight(w):
            dst, outs, ins = weights[w]
            pe.wait_ge(sm["w_step"], WSTEPS * (w + 1))
            pe.wait_ge(sm["sc"], 1)
            for k, os in groups(w):
                n = count[0]
                if n >= 2:
                    pe.wait_ge(sm["wt_lo"], n - 1)
                for e, o in enumerate(os):
                    last = pe.transpose(WT_PS[n % 2][:, e * P:(e + 1) * P],
                                        WN[:, w, (o * ins + k) * P:(o * ins + k + 1) * P], CST[:, C_ID:C_ID + P])
                last.then_inc(sm["wt_ps"], 1)
                count[0] += 1

        def spread(q):
            if count[0]:
                pe.wait_ge(sm["wt_lo"], count[0])
            pe.wait_ge(sm["acol"], q + 1)
            pe.transpose(M_PS[0:1, 0:P], AC[:, q:q + 1], CST[:, C_ID:C_ID + P]).then_inc(sm["am_ps"], 1)
            pe.wait_ge(sm["am1"], q + 1)
            if q:
                pe.wait_ge(sm["sc"], SSTEPS * (q - 1) + 1)
            pe.matmul(M2_PS[:, 0:1], ONE[:, :], A1[0:1, q:q + 1], start=True, stop=True).then_inc(sm["ab_ps"], 1)

        pe.wait_ge(sm["const"], 4)
        spread(0)
        for t in range(TILES):
            pe.wait_ge(sm["xr"], t + 1)
            if t % 2 == 0 and t >= 4:
                pe.wait_ge(sm["xt_lo"], t // 2 - 1)
            for k in range(KT):
                last = pe.transpose(W_PS[2 + t // 2 % 2][:, (2 * k + t % 2) * P:(2 * k + t % 2 + 1) * P],
                                    XN[:, t, k * P:(k + 1) * P], CST[:, C_ID:C_ID + P])
            last.then_inc(sm["xt_ps"], 1)

        def inner(wt, ps, i):
            f, c = i // 4, i % 4
            parts = [(wt[0], XT_HI), (wt[0], XT_LO), (wt[1], XT_HI)]
            for e, (a, k) in enumerate([(x, k) for x in parts for k in range(KT)]):
                last = pe.matmul(W_PS[i % 6][:, :], a[0][:, k, f * P:(f + 1) * P], a[1][:, k, c * CH:(c + 1) * CH],
                                 start=(e == 0), stop=(e == 5))
            last.then_inc(ps, 1)

        turn_weight(0)
        pe.wait_ge(sm["wt_lo"], WT_DONE[0])
        for i in range(CHUNKS):
            if i == 0:
                pe.wait_ge(sm["xt_lo"], TILES // 2)
            if i in TURN:
                turn_weight(TURN[i])
            if i >= 6:
                pe.wait_ge(sm["up_sb"], i - 5)
            inner(WUT, sm["up_ps"], i)
        pe.wait_ge(sm["wt_lo"], WT_DONE[1])
        for i in range(CHUNKS):
            if i < 6:
                pe.wait_ge(sm["up_sb"], CHUNKS - 5 + i)
            else:
                pe.wait_ge(sm["ga_sb"], i - 5)
            if i == U_SCALED:
                spread(1)
            inner(WGT, sm["ga_ps"], i)
        pe.wait_ge(sm["ga_sb"], CHUNKS)
        spread(2)
        spread(3)
        spread(4)
        for t in range(TILES):
            pe.wait_ge(sm["oi"], OUT_TURN[t])
            if t >= 6:
                pe.wait_ge(sm["dn_sb"], t - 5)
            parts = [(0, WDT[0]), (0, WDT[1]), (1, WDT[0])]
            for e, (a, f) in enumerate([(x, f) for f in range(FT) for x in parts]):
                last = pe.matmul(W_PS[t % 6][:, 0:D], GS[:, a[0], f, t * P:(t + 1) * P], a[1][:, f, :],
                                 start=(e == 0), stop=(e == 3 * FT - 1))
            last.then_inc(sm["dn_ps"], 1)

    @block.scalar
    def _(act):
        count = [0]

        def keep_weight(w):
            dst, outs, ins = weights[w]
            for k, os in groups(w):
                n = count[0]
                act.wait_ge(sm["wt_ps"], n + 1)
                nc.scalar.activation(dst[0][:, k, os[0] * P:(os[-1] + 1) * P], WT_PS[n % 2][:, 0:len(os) * P], ACT.Copy,
                                     scale=W_SCALE).then_inc(sm["wt_hi"], 1)
                count[0] += 1

        act.wait_ge(sm["ln3"], LN_ROOT)
        nc.scalar.activation(SD[:, :], VE[:, :], ACT.Sqrt).then_inc(sm["root3"], 1)
        act.wait_ge(sm["ln3"], LN_STEPS)
        for i in range(TILES):
            nc.scalar.activation(XN[:, i, :], X[:, i, :], ACT.Identity, bias=VT[:, i:i + 1], scale=RS[:, i:i + 1])\
                .then_inc(sm["xn3"], 1)
        act.wait_ge(sm["const"], 4)
        for v in range(TILES // 2):
            act.wait_ge(sm["xt_ps"], 2 * v + 2)
            nc.scalar.activation(XT_HI[:, :, 2 * v * P:(2 * v + 2) * P], W_PS[2 + v % 2][:, :].rearrange("p (k r) -> p k r", k=KT),
                                 ACT.Identity, bias=RND[:, 1:2]).then_inc(sm["xt_hi"], 1)
        keep_weight(0)
        for i in range(CHUNKS):
            if i in TURN:
                keep_weight(TURN[i])
            act.wait_ge(sm["up_ps"], i + 1)
            nc.scalar.activation(unit(U, i), W_PS[i % 6][:, :], ACT.Copy, scale=1 / W_SCALE).then_inc(sm["up_sb"], 1)
        for i in range(CHUNKS):
            act.wait_ge(sm["ga_ps"], i + 1)
            nc.scalar.activation(unit(G, i), W_PS[i % 6][:, :], ACT.Copy, scale=1 / W_SCALE).then_inc(sm["ga_sb"], 1)
            if i in U_STEPS:
                f = U_STEPS[i]
                act.wait_ge(sm["scale"], 2)
                nc.scalar.activation(U[:, f, :], U[:, f, :], ACT.Identity, bias=RND[:, 0:1], scale=INV[:, 1:2])\
                    .then_inc(sm["ur"], 1)
        act.wait_ge(sm["gm"], CHUNKS)
        act.wait_ge(sm["scale"], 3)

        def gate_steps(f):
            nc.scalar.activation(G[:, f, :], G[:, f, :], ACT.Identity, bias=RND[:, 0:1], scale=INV[:, 2:3]).then_inc(sm["gr"], 1)

        gate_steps(1)
        for f in range(FT):
            act.wait_ge(sm["gi"], f + 1)
            if f >= 3:
                act.wait_ge(*gate_done(f - 3))
            nc.scalar.activation(SG[:, f % 3, :], G[:, f, :], ACT.Sigmoid, scale=SC[:, 2:3]).then_inc(sm["sg1"], 1)
            act.wait_ge(sm["sg1"], f + 1)
            nc.scalar.activation(SG[:, f % 3, :], SG[:, f % 3, :], ACT.Identity, bias=RND[:, 0:1], scale=U16).then_inc(sm["sg2"], 1)
            if f + 3 < FT and f + 3 not in STEPS_ON_DVE:
                gate_steps(f + 3)
        act.wait_ge(sm["g2m"], FT)
        act.wait_ge(sm["scale"], 4)
        for f in range(FT):
            nc.scalar.activation(G[:, f, :], G[:, f, :], ACT.Identity, bias=RND[:, 0:1], scale=INV[:, 3:4]).then_inc(sm["g2r"], 1)
            if f in OUT_ON_POOL:
                act.wait_ge(sm["g2r"], f + 1)
                nc.scalar.activation(G[:, f, :], G[:, f, :], ACT.Identity, bias=RND[:, 1:2]).then_inc(sm["g2i"], 1)
        act.wait_ge(sm["om"], FT)
        act.wait_ge(sm["scale"], 5)
        for lo, hi in OUT_COLS:
            cols = slice(lo, hi)
            nc.scalar.activation(G[:, :, cols], G[:, :, cols], ACT.Identity, bias=RND[:, 0:1], scale=INV[:, 4:5])\
                .then_inc(sm["or_"], 1)

    @block.vector
    def _(dve):
        dve.memset(ONE[:, :], 1.0).then_inc(sm["const"], 1)
        dve.memset(RND[:, 0:1], ROUND).then_inc(sm["const"], 1)
        dve.memset(RND[:, 1:2], -ROUND).then_inc(sm["const"], 1)
        dve.memset(WORTH[:, 0:1], 1.0).then_inc(sm["const"], 1)
        deviations(dve, sb["STAT"], MV, VE[:, :], SD[:, :], RS[:, :], VT[:, :], sm["ln3"], sm["root3"])

        def weight_scales(w):
            dve.wait_ge(in_wn[w], 16)
            dve.tensor_reduce(WS[:, w, :], WN[:, w, :].rearrange("p (b e) -> p b e", e=WBLOCK), AX.X, ALU.max,
                              apply_absolute_value=True).then_inc(sm["w_max"], 1)
            dve.wait_ge(sm["w_max"], 3 * w + 1)
            dve.tensor_scalar(WS[:, w, :], WS[:, w, :], 1 / W_MAX, TINY, ALU.mult, ALU.max).then_inc(sm["w_max"], 1)
            dve.wait_ge(sm["w_max"], 3 * w + 2)
            dve.reciprocal(WI[:, w, :], WS[:, w, :]).then_inc(sm["w_max"], 1)

        weight_scales(0)
        weight_scales(1)
        for i in range(4):
            dve.wait_ge(sm["xn3"], 4 * i + 4)
            dve.tensor_reduce(AM[:, 0, i:i + 1], XN[:, 4 * i:4 * i + 4, :].rearrange("p t d -> p (t d)"), AX.X, ALU.max,
                              apply_absolute_value=True).then_inc(sm["xm"], 1)
        dve.wait_ge(sm["xm"], 4)
        dve.tensor_reduce(AC[:, 0:1], AM[:, 0, 0:4], AX.X, ALU.max).then_inc(sm["acol"], 1)

        def scales(q, worth=None):
            n = SSTEPS * q
            if worth is not None:
                worth(WORTH[:, q:q + 1]).then_inc(sm["const"], 1)
            dve.wait_ge(sm["const"], 4 + q)
            dve.wait_ge(sm["am_ps"], q + 1)
            dve.tensor_reduce(A1[0:1, q:q + 1], M_PS[0:1, 0:P], AX.X, ALU.max).then_inc(sm["am1"], 1)
            dve.wait_ge(sm["ab_ps"], q + 1)
            col = slice(q, q + 1)
            dve.tensor_scalar(SC[:, col], M2_PS[:, 0:1], WORTH[:, col], None, ALU.mult).then_inc(sm["sc"], 1)
            dve.wait_ge(sm["sc"], n + 1)
            dve.tensor_scalar(SC[:, col], SC[:, col], 1 / A_MAX, TINY, ALU.mult, ALU.max).then_inc(sm["sc"], 1)
            dve.wait_ge(sm["sc"], n + 2)
            dve.reciprocal(INV[:, col], SC[:, col]).then_inc(sm["sc"], 1)
            dve.wait_ge(sm["sc"], n + 3)
            dve.tensor_tensor(INV[:, col], INV[:, col], WORTH[:, col], ALU.mult).then_inc(sm["sc"], 2)
            dve.wait_ge(sm["sc"], n + 5)
            dve.tensor_copy(A1[0:1, col], A1[0:1, col]).then_inc(sm["scale"], 1)

        scales(0)
        for t in range(TILES):
            dve.tensor_scalar(XN[:, t, :], XN[:, t, :], INV[:, 0:1], ROUND, ALU.mult, ALU.add).then_inc(sm["xr"], 1)
        for v in range(TILES // 2):
            cols = slice(2 * v * P, (2 * v + 2) * P)
            dve.wait_ge(sm["xt_hi"], v + 1)
            dve.scalar_tensor_tensor(XT_LO[:, :, cols], W_PS[2 + v % 2][:, :].rearrange("p (k r) -> p k r", k=KT), ROUND,
                                     XT_HI[:, :, cols], ALU.subtract, ALU.subtract).then_inc(sm["xt_lo"], 1)
        count = [0]

        def weight_low(w):
            dst = weights[w][0]
            for k, os in groups(w):
                n = count[0]
                cols = slice(os[0] * P, (os[-1] + 1) * P)
                dve.wait_ge(sm["wt_hi"], n + 1)
                dve.scalar_tensor_tensor(dst[1][:, k, cols], WT_PS[n % 2][:, 0:len(os) * P], W_SCALE, dst[0][:, k, cols],
                                         ALU.mult, ALU.subtract).then_inc(sm["wt_lo"], 1)
                count[0] += 1

        weight_low(0)
        weight_scales(2)

        def maxima(src, q, done, landed):
            for i in range(CHUNKS):
                if q == 1 and i in TURN:
                    weight_low(TURN[i])
                if q == 2 and i in U_WHOLE:
                    f = U_WHOLE[i]
                    dve.wait_ge(sm["ur"], f + 1)
                    dve.tensor_scalar(U[:, f, :], U[:, f, :], ROUND, None, ALU.subtract).then_inc(sm["ui"], 1)
                dve.wait_ge(landed, i + 1)
                dve.tensor_reduce(AM[:, q, i:i + 1], unit(src, i), AX.X, ALU.max, apply_absolute_value=True).then_inc(done, 1)
            dve.wait_ge(done, CHUNKS)
            dve.tensor_reduce(AC[:, q:q + 1], AM[:, q, 0:CHUNKS], AX.X, ALU.max).then_inc(sm["acol"], 1)

        def worth_of_input(out):
            return dve.tensor_copy(out, SC[:, 0:1])

        maxima(U, 1, sm["um"], sm["up_sb"])
        scales(1, worth_of_input)
        maxima(G, 2, sm["gm"], sm["ga_sb"])
        scales(2, worth_of_input)

        def gate_whole(f):
            if f in STEPS_ON_DVE:
                dve.tensor_scalar(G[:, f, :], G[:, f, :], INV[:, 2:3], ROUND, ALU.mult, ALU.add).then_inc(sm["grv"], 1)
                dve.wait_ge(sm["grv"], STEPS_ON_DVE.index(f) + 1)
            else:
                dve.wait_ge(sm["gr"], sum(x not in STEPS_ON_DVE for x in range(f + 1)))
            dve.tensor_scalar(G[:, f, :], G[:, f, :], ROUND, None, ALU.subtract).then_inc(sm["gi"], 1)

        def gate_max(f):
            dve.wait_ge(*gate_done(f))
            dve.tensor_reduce(AM[:, 3, f:f + 1], G[:, f, :], AX.X, ALU.max, apply_absolute_value=True).then_inc(sm["g2m"], 1)

        gate_whole(0)
        gate_whole(1)
        gate_whole(2)
        for f in range(FT):
            s = SG[:, f % 3, :]
            dve.wait_ge(sm["sg2"], f + 1)
            dve.tensor_scalar(s, s, ROUND + U16 - 1, ROUND, ALU.min, ALU.subtract).then_inc(sm["sg3"], 1)
            if f not in ON_POOL:
                dve.wait_ge(sm["sg3"], f + 1)
                dve.tensor_tensor(G[:, f, :], G[:, f, :], s, ALU.mult).then_inc(sm["g2v"], 1)
            if f + 3 < FT:
                gate_whole(f + 3)
            if f:
                gate_max(f - 1)
        gate_max(FT - 1)
        dve.wait_ge(sm["g2m"], FT)
        dve.tensor_reduce(AC[:, 3:4], AM[:, 3, 0:FT], AX.X, ALU.max).then_inc(sm["acol"], 1)
        scales(3, lambda out: dve.tensor_scalar(out, SC[:, 2:3], 1 / U16, None, ALU.mult))
        def out_max(f):
            if f in OUT_ON_POOL:
                dve.wait_ge(sm["o_p"], OUT_ON_POOL.index(f) + 1)
            else:
                dve.wait_ge(sm["o_v"], sum(x not in OUT_ON_POOL for x in range(f + 1)))
            dve.tensor_reduce(AM[:, 4, f:f + 1], G[:, f, :], AX.X, ALU.max, apply_absolute_value=True).then_inc(sm["om"], 1)

        dve.wait_ge(sm["ui"], FT)
        for f in range(FT):
            if f not in OUT_ON_POOL:
                dve.wait_ge(sm["g2r"], f + 1)
                dve.scalar_tensor_tensor(G[:, f, :], G[:, f, :], ROUND, U[:, f, :], ALU.subtract, ALU.mult).then_inc(sm["o_v"], 1)
            if f >= 2:
                out_max(f - 2)
        out_max(FT - 2)
        out_max(FT - 1)
        dve.wait_ge(sm["om"], FT)
        dve.tensor_reduce(AC[:, 4:5], AM[:, 4, 0:FT], AX.X, ALU.max).then_inc(sm["acol"], 1)
        scales(4, lambda out: dve.tensor_tensor(out, SC[:, 3:4], SC[:, 1:2], ALU.mult))
        dve.tensor_scalar(SCD, SC[:, 4:5], 1 / W_SCALE, None, ALU.mult).then_inc(sm["const"], 1)
        for c, (lo, hi) in enumerate(OUT_COLS):
            cols = slice(lo, hi)
            dve.wait_ge(sm["or_"], c + 1)
            dve.tensor_scalar(GS[:, 0, :, cols], G[:, :, cols], ROUND, None, ALU.subtract).then_inc(sm["oh"], 1)
            dve.wait_ge(sm["oh"], c + 1)
            dve.scalar_tensor_tensor(GS[:, 1, :, cols], G[:, :, cols], ROUND, GS[:, 0, :, cols], ALU.subtract, ALU.subtract)\
                .then_inc(sm["oi"], 1)
        dve.wait_ge(sm["const"], 9)
        for t in range(TILES):
            dve.wait_ge(sm["dn_ps"], t + 1)
            dve.scalar_tensor_tensor(X[:, t, :], W_PS[t % 6][:, 0:D], SCD, X[:, t, :], ALU.mult, ALU.add)\
                .then_inc(sm["dn_sb"], 1)




def program(nc, out, **dram):
    with ExitStack() as top:
        kmask = nc.dram_tensor("kmask", (B, LK), F16).ap()
        sb = {"X": top.enter_context(nc.sbuf_tensor("X", [P, TILES, D], F32)),
              "CST": top.enter_context(nc.sbuf_tensor("CST", [P, C_ALL], F32)),
              "STAT": top.enter_context(nc.sbuf_tensor("STAT", [P, TILES, 6], F32))}
        dram = dict(dram, kmask=kmask, out=out)
        with ExitStack() as ctx:
            cross_attention(nc, sb, ctx, dram)
        with ExitStack() as ctx:
            self_attention(nc, sb, ctx, dram)
        with ExitStack() as ctx:
            feed_forward(nc, sb, ctx, dram)


def projection_rows(w):
    rows = np.zeros((4, 32, 4, D), w.dtype)
    rows[:, :DH] = w.T.reshape(4, 4, DH, D).transpose(1, 2, 0, 3)
    return rows.reshape(P, 4, D)


def position_bias(rpb):
    index = np.arange(SQ)[None, :] - np.arange(SQ)[:, None] + SQ - 1
    return np.ascontiguousarray(rpb[index].reshape(SQ, SQ, PAIRS, 2).transpose(3, 0, 2, 1).reshape(P, PAIRS, SQ))


def arrays_of(inp):
    c = np.ascontiguousarray
    return dict(
        x=c(np.asarray(inp["x"]).reshape(ROWS, D)),
        ctx_t=c(np.asarray(inp["ctx_1024"]).transpose(0, 2, 1)),
        lens=c(np.asarray(inp["_lenS2"]).reshape(1, B)),
        wk_t=c(np.asarray(inp["L0_xattn_Wk"]).T), bk=c(np.asarray(inp["L0_xattn_bk"]).reshape(KT, P).T),
        wq_t=c(np.asarray(inp["L0_xattn_Wq"]).T), bq=c(np.tile(np.asarray(inp["L0_xattn_bq"]).reshape(PAIRS, 32).T, (4, 1))),
        wv_t=c(np.asarray(inp["L0_xattn_Wv"]).T), bv=c(inp["L0_xattn_bv"]),
        w_t=c(np.asarray(inp["L0_attn_W_w"]).T),
        bqk=c(np.asarray(inp["L0_attn_W_b"])[:2 * D].reshape(4, P).T), bv2=c(np.asarray(inp["L0_attn_W_b"])[2 * D:]),
        bp=c(inp["L0_attn_proj_b"]), ln_g=c(inp["L0_attn_ln_g"]), ln_b=c(inp["L0_attn_ln_b"]),
        wp=projection_rows(np.asarray(inp["L0_attn_proj_w"])), bias=position_bias(np.asarray(inp["L0_attn_rpb"])),
        w_up=c(inp["L0_ffn_w_up"]), w_gate=c(inp["L0_ffn_w_gate"]), w_down=c(inp["L0_ffn_w_down"]),
        cst=constants(), tok=np.arange(LK, dtype=np.float32).reshape(1, LK))


_OUT = (B, SQ, D)


def kernel(**inputs):
    import concourse.bacc as _bacc
    from concourse.bass_utils import run_bass_kernel_spmd as _run

    nc = _bacc.Bacc("TRN2", target_bir_lowering=False, num_devices=1)
    arrays, aps = {}, {}
    for name, a in arrays_of(inputs).items():
        arrays[f"in_{name}"] = a
        aps[name] = nc.dram_tensor(f"in_{name}", a.shape, mybir.dt.from_np(a.dtype), kind="ExternalInput").ap()
    out = nc.dram_tensor("out", (ROWS, D), F32, kind="ExternalOutput").ap()
    program(nc, out=out, **aps)
    r = _run(nc, [arrays], core_ids=[0])
    return r.results[0]["out"].reshape(_OUT)
```
